# Optimizing a Trainium2 kernel written in Bass

```python
import numpy as np
import jax
import jax.numpy as jnp

def _softmax(x, axis=-1):
    return jax.nn.softmax(x, axis=axis)

def _gelu(x):
    return jax.nn.gelu(x, approximate=True)

def _silu(x):
    return jax.nn.silu(x)

def _sigmoid(x):
    return jax.nn.sigmoid(x)

def _layernorm(x, axis=-1, eps=1e-05):
    m = jnp.mean(x, axis=axis, keepdims=True)
    v = jnp.var(x, axis=axis, keepdims=True)
    return (x - m) / jnp.sqrt(v + eps)

def _scatter_add(tgt, idx, src, axis=0):
    return tgt.at[idx].add(src)

def _segment_sum(src, seg, n):
    return jax.ops.segment_sum(src, seg, n)
kernel_name = 'mk_gnn_resnorm_d1_gnn_r8_d4ac92'

def setup_inputs(seed: int=0):
    np.random.seed(seed)
    _w = jnp.asarray

    def _rec_inputs():
        import jax
        import jax.numpy as jnp
        _gk = jax.random.key(seed)
        x = -6.415e-05 + 1 * jax.random.normal(jax.random.fold_in(_gk, 1), (6250, 512), jnp.float32)
        _s = jax.random.randint(jax.random.fold_in(_gk, 2), (50000,), 0, 6250, jnp.int32)
        _d = jax.random.randint(jax.random.fold_in(_gk, 3), (50000,), 0, 6250, jnp.int32)
        _loop = jnp.arange(6250, dtype=jnp.int32)
        src = jnp.concatenate([_s, _d, _loop])
        dst = jnp.concatenate([_d, _s, _loop])
        _o = jnp.argsort(dst, stable=True)
        src = src[_o]
        dst = dst[_o]
        edge_type_8 = jax.random.randint(jax.random.fold_in(_gk, 12), (106250,), 0, 8, jnp.int32)
        return (x, src, dst, edge_type_8)
    x, src, dst, edge_type_8 = _rec_inputs()

    def _L0_gnn_setup():
        import jax, jax.numpy as jnp
        import numpy as np
        N_NODES = 2500
        N_EDGES = 40000
        N_REL = 8
        D_IN = 512
        D_OUT = 512
        key = jax.random.key(seed)
        k1, k2, k3, k4, k5 = jax.random.split(key, 5)
        x = jax.random.normal(k1, (N_NODES, D_IN), dtype=jnp.float32)
        W_self = jax.random.normal(k2, (D_OUT, D_IN), dtype=jnp.float32) * 0.05
        W_rel = jax.random.normal(k3, (N_REL, D_OUT, D_IN), dtype=jnp.float32) * 0.05
        bias = jnp.zeros((D_OUT,), dtype=jnp.float32)
        edge_index = jax.random.randint(k4, (2, N_EDGES), 0, N_NODES, dtype=jnp.int64)
        edge_type = jax.random.randint(k5, (N_EDGES,), 0, N_REL, dtype=jnp.int64)
        return {'x': x, 'W_self': W_self, 'W_rel': W_rel, 'bias': bias, 'edge_index': edge_index, 'edge_type': edge_type}
    _L0_gnn_all = _L0_gnn_setup()
    _L0_gnn_in = {k: v for k, v in _L0_gnn_all.items() if k in ('W_self', 'W_rel', 'bias')}
    del _L0_gnn_all
    return {'x': x, 'src': src, 'dst': dst, 'edge_type_8': edge_type_8, 'L0_gnn_W_self': _L0_gnn_in['W_self'], 'L0_gnn_W_rel': _L0_gnn_in['W_rel'], 'L0_gnn_bias': _L0_gnn_in['bias']}

def reference(x, src, dst, edge_type_8, L0_gnn_W_self, L0_gnn_W_rel, L0_gnn_bias):
    import jax
    import jax.numpy as jnp

    def _L0_gnn_ref(x, W_self, W_rel, bias, edge_index, edge_type):
        import jax, jax.numpy as jnp
        import numpy as np
        N_NODES = 2500
        N_EDGES = 40000
        N_REL = 8
        D_IN = 512
        D_OUT = 512
        N = x.shape[0]
        R, d_out, _ = W_rel.shape
        src, dst = (edge_index[0], edge_index[1])
        out = jnp.einsum('ni,oi->no', x, W_self)
        h_rel = jnp.einsum('ni,roi->rno', x, W_rel)
        msg = h_rel[edge_type, src]
        seg = edge_type * N + dst
        agg = jax.ops.segment_sum(msg, seg, num_segments=R * N).reshape(R, N, d_out)
        cnt = jax.ops.segment_sum(jnp.ones((msg.shape[0],), dtype=x.dtype), seg, num_segments=R * N).reshape(R, N, 1)
        cnt = jnp.maximum(cnt, 1.0)
        out = out + jnp.sum(agg / cnt, axis=0)
        return out + bias
    edge_index = jnp.stack([src, dst])
    x = _layernorm(x + _L0_gnn_ref(x, L0_gnn_W_self, L0_gnn_W_rel, L0_gnn_bias, edge_index, edge_type_8), axis=-1)
    return x

_drawn_inputs = setup_inputs


def setup_inputs(seed=0):
    import zlib

    import numpy as np

    out = dict(_drawn_inputs(seed))
    spreads = {'L0_gnn_bias': (0.0, 0.1)}
    factors = {}
    for name, (base, spread) in spreads.items():
        noise = np.random.default_rng([zlib.crc32(name.encode()), seed]).standard_normal(out[name].shape)
        drawn = base * np.exp(spread * noise) if base else spread * noise
        out[name] = jnp.asarray(drawn.astype(out[name].dtype))
    for name, factor in factors.items():
        out[name] = (out[name] * factor).astype(out[name].dtype)
    return out
```

```python
import concourse.bass as bass
from concourse import mybir
from contextlib import ExitStack


def build_gnn(nc, x, src, dst, etype, w_self, w_rel, bias, out):
    f32, f16, i32 = mybir.dt.float32, mybir.dt.float16, mybir.dt.int32
    ALU, ACT, AX = mybir.AluOpType, mybir.ActivationFunctionType, mybir.AxisListType
    ds = bass.ds

    P = 128
    N, D = x.shape
    R = w_rel.shape[0]
    E = src.shape[0]
    KB = D // P
    NT = -(-N // P)
    LAST = N - (NT - 1) * P
    PAIRS = (NT - 1) // 2
    C = -(-E // P)
    C = -(-C // NT) * NT
    SC = C // NT
    E_LAST = E - (P - 1) * C
    KPT = 3
    SORT_PAIRS = -(-(NT + 1) // (2 * KPT))
    K = SORT_PAIRS * 2 * KPT
    CPT = -(-((E + NT * (P - 1)) // P) // NT)
    NCH = CPT * NT
    HALF = CPT // 2
    CG = -(-(NCH + 3) // P)
    NCP = CG * P
    INVALID = float(P << 16)
    EPS = 1e-5
    SX, SW, SH, SWT = 2.0 ** 6, 2.0 ** 10, 2.0 ** 6, 2.0 ** 10
    assert E_LAST > 0 and 2 * PAIRS + 1 == NT and CPT % 6 == 0 and K * P < 2 ** 16

    h = nc.dram_tensor("h_parts", [N * R, 2 * D], f16, kind="Internal").ap()
    h_rows = h.rearrange("(n r) d -> n (r d)", r=R)
    slots = nc.dram_tensor("sorted_records", [NCP * P, 1], f32, kind="Internal").ap()
    rowids = nc.dram_tensor("sorted_rows", [NCP * P], f16, kind="Internal").ap()

    ctx = ExitStack()
    with ctx:
        def sb(name, shape, dt):
            return ctx.enter_context(nc.sbuf_tensor(name, shape, dt))

        def sem(name):
            return ctx.enter_context(nc.semaphore(name))

        wrel = sb("wrel", [P, R, KB, 2, D], f16)
        wself = sb("wself", [P, KB, 2, D], f16)
        xst = sb("xst", [P, 2, D], f32)
        xT = sb("xT", [P, 2, 2, KB * P], f16)
        arena = sb("arena", [P, NT * D], f32)
        gidx = sb("gidx", [P, NCP], i32)
        rowT = sb("rowT", [P, NCP], f32)
        wgt = sb("wgt", [P, NCP, 2], f32)
        onehot = sb("onehot", [P, 6, 2, P], f16)
        tile_i = sb("tile_i", [1, NCP], i32)
        ident = sb("ident", [P, P], f32)
        before = sb("before", [P, P], f32)
        ones = sb("ones", [P, P], f32)
        iota_row = sb("iota_row", [P, P], f16)
        iota_part = sb("iota_part", [P, 1], f32)
        iota_k = sb("iota_k", [P, K], f32)
        idx_a = sb("idx_a", [P, max(SC, CPT)], i32)
        rec_a = sb("rec_a", [P, SC], f32)
        biasb = sb("biasb", [P, D], f32)
        stats = sb("stats", [P, 2, 6], f32)
        mv = sb("mv", [P, NT, 2], f32)
        hist = sb("hist", [P, K], f32)
        total = sb("total", [P, K], f32)
        total_i = sb("total_i", [P, K], i32)
        nchunk = sb("nchunk", [P, K], f32)
        cend = sb("cend", [P, K], f32)
        base = sb("base", [P, K], f32)
        onesk = sb("onesk", [P, K], f32)

        acc = arena[:, :].rearrange("p (t d) -> p t d", d=D)
        used = [0]

        def view(n, dt, at=None):
            size = {f32: 4, i32: 4, f16: 2}[dt] * n
            start = used[0] if at is None else at
            used[0] = max(used[0], start + size)
            assert start % 4 == 0 and size % 4 == 0 and used[0] <= NT * D * 4, (start, size)
            v = arena[:, start // 4:(start + size) // 4]
            return v if dt == f32 else v.bitcast(dt)

        hst = view(2 * R * 2 * D, f16).rearrange("p (j r c d) -> p j r c d", j=2, r=R, c=2)
        wst = view(2 * KB * D, f32, at=0).rearrange("p (j b i) -> p j b i", j=2, b=KB)
        edges_at = used[0]
        key = view(-(-C // 2) * 2, f16)[:, 0:C]
        onek = view(-(-C // 2) * 2, f16)[:, 0:C]
        cum = view(-(-C // 2) * 2, f16)[:, 0:C]
        onesc = view(-(-C // 2) * 2, f16)[:, 0:C]
        pos = view(C, f32)
        rec = view(C, f32)
        val = view(C, f32)
        dst_i = view(C, i32)
        src_i = view(C, i32)
        et_i = view(C, i32)
        tmp_i = view(C, i32)
        pos_i = view(C, i32)
        cidx = view(NCP, f32)
        tiles = view(NCP, f32)
        same_prev = view(NCP, f32)
        same_next = view(NCP, f32)
        cnt = view(R * NCP, f32, at=0).rearrange("p (r c) -> p r c", r=R)
        run = view(R * NCP, f32, at=edges_at).rearrange("p (r c) -> p r c", r=R)
        inv = view(2 * R * NCP, f16, at=edges_at).rearrange("p (q c) -> p q c", q=2 * R)
        D1 = view(2 * HALF * P, f16).rearrange("p (j c d) -> p j c d", j=2, c=HALF)
        DT = view(2 * HALF * P, f16).rearrange("p (j c d) -> p j c d", j=2, c=HALF)
        rows_b = view(2 * HALF * P, f16).rearrange("p (j c d) -> p j c d", j=2, c=HALF)
        relT = view(NCP, f32)
        wrel_pad = wrel[:, 0].rearrange("p k a d -> p (k a d)").bitcast(f32)[:, 0:NCP]
        slotc = wrel[:, 0].rearrange("p k a d -> p (k a d)").bitcast(f32)[:, 0:CG * P]
        slotc_i = wrel[:, 1].rearrange("p k a d -> p (k a d)").bitcast(i32)[:, 0:CG * P]
        rowc = wrel[:, 2].rearrange("p k a d -> p (k a d)")[:, 0:CG * P]
        rec_i = wrel[:, 3].rearrange("p k a d -> p (k a d)").bitcast(i32)[:, 0:NCP]
        t_i = wrel[:, 4].rearrange("p k a d -> p (k a d)").bitcast(i32)[:, 0:NCP]
        rel1 = wrel[:, 5:7].rearrange("p r k a d -> p (r k a d)")[:, 0:NCP * R].rearrange(
            "p (c r) -> p c r", r=R)
        prod = wrel[:, 7].rearrange("p k a d -> p (k a d)").bitcast(f32)[:, 0:HALF * 2 * R].rearrange(
            "p (c q r) -> p c q r", q=2, r=R)
        gath = wrel[:, 0:2].rearrange("p r k a d -> p (r k a d)")[:, 0:6 * 2 * D].rearrange(
            "p (b q d) -> p b q d", b=6, q=2)

        psT = [ctx.enter_context(nc.psum_tensor(f"psT{j}", [P, D], f32)) for j in range(2)]
        psH = [ctx.enter_context(nc.psum_tensor(f"psH{j}", [P, D], f32)) for j in range(4)]
        psM = [ctx.enter_context(nc.psum_tensor(f"psM{j}", [P, D], f32)) for j in range(2)]

        s_const = sem("consts_made")
        s_edges = sem("edges_loaded")
        s_blank = sem("edge_buffers_padded")
        s_prefill = sem("slots_prefilled")
        s_padrow = sem("pad_records_made")
        s_padrow0 = sem("matrices_cleared")
        s_iota = sem("iotas_made")
        s_slotd = sem("records_decoded")
        s_bias = sem("bias_loaded")
        s_w = [sem(f"w_loaded{j}") for j in range(2)]
        s_wT = sem("w_transposed")
        s_whi = sem("w_high_made")
        s_wlo = sem("w_low_made")
        s_hist = sem("hist_made")
        s_tot = sem("totals_summed")
        s_dve = sem("dve_step")
        s_x = [sem(f"x_loaded{j}") for j in range(2)]
        s_xT = sem("x_transposed")
        s_xhi = sem("x_high_made")
        s_xlo = sem("x_low_made")
        s_h = sem("h_summed")
        s_hhi = sem("h_high_made")
        s_hlo = sem("h_low_made")
        s_st = [sem(f"h_stored{j}") for j in range(2)]
        s_pos = sem("positions_ready")
        s_stage = sem("scatter_staged")
        s_sc = [sem(f"scattered{j}") for j in range(SC)]
        s_slots = sem("slots_complete")
        s_slotl = sem("slots_loaded")
        s_slotT = sem("slots_transposed")
        s_rowc = sem("rowc_made")
        s_rowst = sem("rowids_stored")
        s_D1 = sem("rows_one_hot_made")
        s_cnt = sem("chunk_counted")
        s_cntc = sem("count_copied")
        s_inv = sem("inverse_made")
        s_rb = [sem(f"rows_broadcast{j}") for j in range(2)]
        s_DT = sem("DT_made")
        s_look = sem("weights_looked_up")
        s_w8 = sem("weights_made")
        s_accz = sem("acc_initialised")
        s_idx = sem("indices_staged")
        s_g = [sem(f"gathered{b}") for b in range(6)]
        s_S = sem("one_hots_made")
        s_mm = sem("chunk_summed")
        s_acc = sem("chunk_added")
        s_x2 = sem("x_reloaded")
        s_x2T = sem("x2_transposed")
        s_x2hi = sem("x2_high_made")
        s_x2lo = sem("x2_low_made")
        s_self = sem("self_summed")
        s_own = sem("self_landed")
        s_stats = sem("statistics_landed")
        s_go = sem("pool_waits_passed")
        s_selfa = sem("self_added")
        s_mv = sem("moments_made")
        s_std = sem("deviation_made")
        s_y = sem("normalised")
        s_out = sem("out_stored")

        block = ctx.enter_context(nc.Block())

        def flat(t):
            return t.rearrange("p a b -> p (a b)")

        @block.sync
        def _(sp):
            sp.wait_ge(s_blank, 1)
            for arr, buf in ((dst, dst_i), (src, src_i), (etype, et_i)):
                sp.dma_start(buf[0:P - 1, :], arr[0:(P - 1) * C].rearrange("(p c) -> p c", c=C)).then_inc(s_edges, 16)
                sp.dma_start(buf[P - 1:P, 0:E_LAST], arr[(P - 1) * C:E].rearrange("(p c) -> p c", p=1)).then_inc(s_edges, 16)
            sp.dma_start(biasb[:], bias.rearrange("(o d) -> o d", o=1).broadcast_to([P, D])).then_inc(s_bias, 16)
            sp.wait_ge(s_padrow, 1)
            sp.dma_start(slots.rearrange("(p c) o -> p (c o)", p=P), wrel_pad).then_inc(s_prefill, 16)
            with sp.Fori(0, R // 2) as u:
                for j in range(2):
                    sp.wait_ge(s_wT, KB * (2 * u + j) + KB)
                    sp.dma_start(wst[:, j], w_rel[ds(2 * u + j, 1)].rearrange("r (b p) i -> p (r b) i", p=P)).then_inc(s_w[j], 16)
            sp.wait_ge(s_wT, KB * R + KB)
            sp.dma_start(wst[:, 0], w_self.rearrange("(b p) i -> p b i", p=P)).then_inc(s_w[0], 16)

            def load_x(t, j):
                sp.dma_start(xst[:, j], x[ds(t * P, P), :]).then_inc(s_x[j], 16)

            def store_h(t, j, n=P):
                sp.wait_ge(s_hlo, 4 + R * (t + 1))
                sp.dma_start(h_rows[ds(t * P, n), :],
                             hst[0:n, j].rearrange("p r c d -> p (r c d)")).then_inc(s_st[j], 16)

            load_x(0, 0)
            load_x(1, 1)
            with sp.Fori(0, PAIRS - 1) as u:
                for j in range(2):
                    sp.wait_ge(s_xT, 2 * u + j + 1)
                    load_x(2 * u + j + 2, j)
                    store_h(2 * u + j, j)
            sp.wait_ge(s_xT, NT - 2)
            sp.dma_start(xst[0:LAST, 0], x[(NT - 1) * P:N, :]).then_inc(s_x[0], 16)
            store_h(NT - 3, 0)
            store_h(NT - 2, 1)
            store_h(NT - 1, 0, LAST)
            sp.wait_ge(s_slots, 1)
            sp.wait_ge(s_h, R * NT)
            sp.dma_start(slotc.rearrange("p (g e) -> p g e", g=CG),
                         slots.rearrange("(g p e) o -> p g (e o)", p=P, e=P)).then_inc(s_slotl, 16)
            sp.wait_ge(s_rowc, 1)
            sp.dma_start(rowids.rearrange("(g p e) -> p g e", p=P, e=P),
                         rowc.rearrange("p (g e) -> p g e", g=CG)).then_inc(s_rowst, 16)
            sp.wait_ge(s_rowst, 16)
            with sp.Fori(0, NT) as i:
                for j in range(2):
                    sp.wait_ge(s_DT, 2 * i + j + 1)
                    sp.dma_start(rows_b[:, j].rearrange("p c d -> p (c d)"),
                                 rowids[ds((2 * i + j) * (HALF * P), HALF * P)].rearrange("(o e) -> o e", o=1)
                                 .broadcast_to([P, HALF * P])).then_inc(s_rb[j], 16)
            with sp.Fori(0, NT - 1) as i:
                sp.wait_ge(s_selfa, i + 1)
                sp.dma_start(xst[:, 0], x[ds(i * P, P), :]).then_inc(s_x2, 16)
            sp.wait_ge(s_selfa, NT)
            sp.dma_start(xst[0:LAST, 0], x[(NT - 1) * P:N, :]).then_inc(s_x2, 16)
            with sp.Fori(0, NT - 1) as i:
                sp.wait_ge(s_y, i + 1)
                sp.dma_start(out[ds(i * P, P), :], flat(acc[:, ds(i, 1), :])).then_inc(s_out, 16)
            sp.wait_ge(s_y, NT)
            sp.dma_start(out[(NT - 1) * P:N, :], acc[0:LAST, NT - 1, :]).then_inc(s_out, 16)
            sp.wait_ge(s_out, 16 * NT)
            sp.wait_ge(s_st[0], 16 * (PAIRS + 1))
            sp.wait_ge(s_st[1], 16 * PAIRS)

        @block.tensor
        def _(pe):
            pe.sem_inc(s_wT, 2 * KB)
            pe.wait_ge(s_const, 6)

            def w_transposes(j, n_w, g):
                pe.wait_ge(s_w[j], 16 * n_w)
                for k in range(KB):
                    pe.wait_ge(s_wlo, g + k + 1)
                    for b in range(KB):
                        last = nc.tensor.transpose(psH[k][:, b * P:(b + 1) * P], wst[:, j, b, k * P:(k + 1) * P], ident[:])
                    last.then_inc(s_wT, 1)

            with pe.Fori(0, R // 2) as u:
                for j in range(2):
                    w_transposes(j, u + 1, (2 * u + j) * KB)
            w_transposes(0, R // 2 + 1, R * KB)
            pe.wait_ge(s_hist, 1)
            nc.tensor.matmul(psM[0][:, 0:K], ones[:], hist[:], start=True, stop=True)
            nc.tensor.matmul(psM[1][:, 0:K], before[:], hist[:], start=True, stop=True).then_inc(s_tot, 1)

            def x_transposes(j, n_x, t):
                pe.wait_ge(s_x[j], 16 * n_x)
                pe.wait_ge(s_xlo, t + 1)
                for k in range(KB):
                    last = nc.tensor.transpose(psT[j][:, k * P:(k + 1) * P], xst[:, j, k * P:(k + 1) * P], ident[:])
                last.then_inc(s_xT, 1)

            def products(bank, j, w):
                for k in range(KB):
                    hi, lo = xT[:, j, 0, k * P:(k + 1) * P], xT[:, j, 1, k * P:(k + 1) * P]
                    nc.tensor.matmul(bank[:], hi, w[:, k, 0, :], start=(k == 0), stop=False)
                    nc.tensor.matmul(bank[:], hi, w[:, k, 1, :], start=False, stop=False)
                    last = nc.tensor.matmul(bank[:], lo, w[:, k, 0, :], start=False, stop=(k == KB - 1))
                return last

            def tile_products(j, t):
                pe.wait_ge(s_xlo, 2 + t + 1)
                for r in range(R):
                    pe.wait_ge(s_hlo, R * t + r + 1)
                    products(psH[r % 4], j, wrel[:, r]).then_inc(s_h, 1)

            pe.wait_ge(s_wlo, KB + KB * (R + 1))
            x_transposes(0, 1, 0)
            with pe.Fori(0, PAIRS) as u:
                x_transposes(1, u + 1, 2 * u + 1)
                tile_products(0, 2 * u)
                x_transposes(0, u + 2, 2 * u + 2)
                tile_products(1, 2 * u + 1)
            tile_products(0, NT - 1)

            pe.wait_ge(s_slotl, 16)
            for g in range(CG):
                last = nc.tensor.transpose(psM[g // 4][:, (g % 4) * P:(g % 4 + 1) * P], slotc[:, g * P:(g + 1) * P], ident[:])
            last.then_inc(s_slotT, 1)
            with pe.Fori(0, NT) as i:
                for j in range(2):
                    pe.wait_ge(s_D1, 2 * i + j + 1)
                    pe.wait_ge(s_cntc, 2 * i + j + 1)
                    for c in range(HALF):
                        last = nc.tensor.matmul(psM[j][:, c * R:(c + 1) * R], D1[:, j, c, :],
                                                flat(rel1[:, ds((2 * i + j) * HALF + c, 1), :]), start=True, stop=True)
                    last.then_inc(s_cnt, 1)
            pe.wait_ge(s_inv, 1)
            with pe.Fori(0, NT) as i:
                for j in range(2):
                    pe.wait_ge(s_DT, 2 + 2 * i + j + 1)
                    pe.wait_ge(s_w8, 2 * i + j + 1)
                    for c in range(HALF):
                        last = nc.tensor.matmul(psM[j][:, c * 2 * R:(c + 1) * 2 * R], DT[:, j, c, :],
                                                inv[:, :, ds((2 * i + j) * HALF + c, 1)].rearrange("p q c -> p (q c)"),
                                                start=True, stop=True)
                    last.then_inc(s_look, 1)
            pe.sem_inc(s_mm, 6)

            def step2(i):
                for s in range(CPT):
                    if s == 4:
                        pe.wait_ge(s_x2, 16 * (i + 1))
                        pe.wait_ge(s_x2lo, i + 1)
                        for k in range(KB):
                            last = nc.tensor.transpose(psT[0][:, k * P:(k + 1) * P], xst[:, 0, k * P:(k + 1) * P], ident[:])
                        last.then_inc(s_x2T, 1)
                    b = s % 6
                    pe.wait_ge(s_g[b], 16 * ((CPT // 6) * i + s // 6 + 1))
                    pe.wait_ge(s_S, CPT * i + s + 1)
                    pe.wait_ge(s_acc, CPT * i + s + 1)
                    bank = psH[s % 3]
                    nc.tensor.matmul(bank[:], onehot[:, b, 0, :], gath[:, b, 0, :], start=True, stop=False)
                    nc.tensor.matmul(bank[:], onehot[:, b, 0, :], gath[:, b, 1, :], start=False, stop=False)
                    nc.tensor.matmul(bank[:], onehot[:, b, 1, :], gath[:, b, 0, :], start=False, stop=True).then_inc(s_mm, 1)
                    if s == 8:
                        pe.wait_ge(s_x2lo, i + 2)
                        pe.wait_ge(s_selfa, i + 1)
                        products(psH[3], 0, wself).then_inc(s_self, 1)

            with pe.Fori(0, NT) as i:
                step2(i)

        @block.scalar
        def _(act):
            def w_high(dest, g, k):
                act.wait_ge(s_wT, 2 * KB + g + k + 1)
                nc.scalar.activation(dest, psH[k][:], ACT.Copy, scale=SW).then_inc(s_whi, 1)

            act.wait_ge(s_prefill, 16)
            with act.Fori(0, R) as r:
                for k in range(KB):
                    w_high(wrel[:, ds(r, 1), k, 0, :].rearrange("p r d -> p (r d)"), r * KB, k)
            for k in range(KB):
                w_high(wself[:, k, 0, :], R * KB, k)

            def x_high(j, t, reused=True):
                act.wait_ge(s_xT, t + 1)
                if reused:
                    act.wait_ge(s_h, R * (t - 1))
                nc.scalar.activation(xT[:, j, 0, :], psT[j][:], ACT.Copy, scale=SX).then_inc(s_xhi, 1)

            def h_high(j, t, reused=True):
                for r in range(R):
                    act.wait_ge(s_h, R * t + r + 1)
                    if r == 0 and reused:
                        act.wait_ge(s_st[j], 8 * (t - j))
                    nc.scalar.activation(hst[:, j, r, 0, :], psH[r % 4][:], ACT.Copy,
                                         scale=SH / (SX * SW)).then_inc(s_hhi, 1)

            x_high(0, 0, reused=False)
            act.wait_ge(s_wlo, KB + KB * (R + 1))
            x_high(1, 1, reused=False)
            h_high(0, 0, reused=False)
            x_high(0, 2)
            h_high(1, 1, reused=False)
            x_high(1, 3)
            h_high(0, 2)
            with act.Fori(1, PAIRS - 1) as u:
                x_high(0, 2 * u + 2)
                h_high(1, 2 * u + 1)
                x_high(1, 2 * u + 3)
                h_high(0, 2 * u + 2)
            x_high(0, NT - 1)
            h_high(1, NT - 2)
            h_high(0, NT - 1)
            act.sem_inc(s_cntc, 2)
            act.wait_ge(s_st[0], 16 * (PAIRS + 1))
            act.wait_ge(s_st[1], 16 * PAIRS)
            with act.Fori(0, NT) as i:
                for j in range(2):
                    act.wait_ge(s_cnt, 2 + 2 * i + j + 1)
                    nc.scalar.activation(cnt[:, :, ds((2 * i + j) * HALF, HALF)],
                                         psM[j][:, 0:HALF * R].rearrange("p (c r) -> p r c", r=R), ACT.Copy).then_inc(s_cntc, 1)
            act.wait_ge(s_bias, 16)
            act.wait_ge(s_w8, 2 + 2 * NT)
            with act.Fori(0, NT) as i:
                nc.scalar.activation(flat(acc[:, ds(i, 1), :]), biasb[:], ACT.Copy).then_inc(s_accz, 1)
            with act.Fori(0, NT) as i:
                act.wait_ge(s_x2T, i + 1)
                act.wait_ge(s_selfa, i + 1)
                nc.scalar.activation(xT[:, 0, 0, :], psT[0][:], ACT.Copy, scale=SX).then_inc(s_x2hi, 1)
            act.wait_ge(s_mv, 1)
            nc.scalar.activation(mv[:, :, 1], mv[:, :, 1], ACT.Sqrt).then_inc(s_std, 1)

        @block.gpsimd
        def _(pool):
            nc.gpsimd.memset(dst_i, NT * P).then_inc(s_const, 1)
            nc.gpsimd.memset(src_i, 0).then_inc(s_const, 1)
            nc.gpsimd.memset(et_i, 0).then_inc(s_const, 1)
            pool.wait_ge(s_const, 3)
            pool.sem_inc(s_blank, 1)
            nc.gpsimd.memset(ident[:], 0.0).then_inc(s_padrow0, 1)
            nc.gpsimd.memset(before[:], 0.0).then_inc(s_padrow0, 1)
            pool.wait_ge(s_padrow0, 2)
            nc.gpsimd.affine_select(out=ident[:], in_=ident[:], compare_op=ALU.not_equal, fill=1.0, base=0,
                                    pattern=[[-1, P]], channel_multiplier=1).then_inc(s_const, 1)
            nc.gpsimd.affine_select(out=before[:], in_=before[:], compare_op=ALU.is_ge, fill=1.0, base=0,
                                    pattern=[[-1, P]], channel_multiplier=1).then_inc(s_const, 1)
            nc.gpsimd.memset(ones[:], 1.0).then_inc(s_const, 1)
            nc.gpsimd.iota(iota_row[:], pattern=[[1, P]], base=0, channel_multiplier=0,
                           allow_small_or_imprecise_dtypes=True).then_inc(s_iota, 1)
            nc.gpsimd.iota(iota_part[:], pattern=[[0, 1]], base=0, channel_multiplier=1,
                           allow_small_or_imprecise_dtypes=True).then_inc(s_iota, 1)
            nc.gpsimd.iota(iota_k[:], pattern=[[1, K]], base=0, channel_multiplier=0,
                           allow_small_or_imprecise_dtypes=True).then_inc(s_iota, 1)
            nc.gpsimd.iota(cidx, pattern=[[1, NCP]], base=0, channel_multiplier=0,
                           allow_small_or_imprecise_dtypes=True).then_inc(s_iota, 1)
            nc.gpsimd.memset(wrel_pad, INVALID).then_inc(s_padrow, 1)
            pool.wait_ge(s_pos, 1)
            pool.wait_ge(s_prefill, 16)

            def scatter(i, first=False):
                for c in range(0 if first else SC):
                    pool.wait_ge(s_sc[c], i * 16)
                nc.gpsimd.tensor_copy(idx_a[:, 0:SC], pos_i[:, ds(i * SC, SC)]).then_inc(s_stage, 1)
                nc.gpsimd.tensor_copy(rec_a[:], rec[:, ds(i * SC, SC)]).then_inc(s_stage, 1)
                pool.wait_ge(s_stage, 2 * i + 2)
                pool.sem_inc(s_go, 1)
                for c in range(SC):
                    nc.gpsimd.indirect_dma_start(
                        out=slots[:, :], out_offset=bass.IndirectOffsetOnAxis(ap=idx_a[:, c:c + 1], axis=0),
                        in_=rec_a[:, c:c + 1], in_offset=None).then_inc(s_sc[c], 16)

            scatter(0, first=True)
            with pool.Fori(1, NT) as i:
                scatter(i)
            for c in range(SC):
                pool.wait_ge(s_sc[c], 16 * NT)
            pool.sem_inc(s_slots, 1)
            pool.wait_ge(s_accz, NT)
            pool.wait_ge(s_st[0], 16 * (PAIRS + 1))
            pool.wait_ge(s_st[1], 16 * PAIRS)

            def step2(i):
                for a in range(2):
                    nc.gpsimd.tensor_copy(idx_a[:, a * HALF:(a + 1) * HALF],
                                          gidx[:, ds(i * CPT + a * HALF, HALF)]).then_inc(s_idx, 1)
                    pool.wait_ge(s_idx, 2 * i + a + 1)
                    for s in range(a * HALF, (a + 1) * HALF):
                        pool.wait_ge(s_mm, CPT * i + s + 1)
                        pool.sem_inc(s_go, 1)
                        nc.gpsimd.indirect_dma_start(
                            out=gath[:, s % 6].rearrange("p q d -> p (q d)"), out_offset=None, in_=h[:, :],
                            in_offset=bass.IndirectOffsetOnAxis(ap=idx_a[:, s:s + 1], axis=0)).then_inc(s_g[s % 6], 16)

            with pool.Fori(0, NT) as i:
                step2(i)

        @block.vector
        def _(dve):
            steps = Steps(dve, s_dve)
            step = steps.step
            V = nc.vector
            dve.sem_inc(s_wlo, KB)
            dve.sem_inc(s_xlo, 2)
            dve.sem_inc(s_hlo, 4)
            dve.sem_inc(s_cnt, 2)
            dve.sem_inc(s_DT, 2)
            dve.sem_inc(s_look, 2)
            dve.sem_inc(s_w8, 2)
            dve.sem_inc(s_acc, 3)
            dve.sem_inc(s_x2lo, 1)
            dve.sem_inc(s_selfa, 1)
            V.memset(onesc, 1.0).then_inc(s_dve, 1)
            V.memset(onesk[:], 1.0).then_inc(s_dve, 1)
            V.memset(pos, 0.0).then_inc(s_dve, 1)
            V.memset(tiles, 0.0).then_inc(s_dve, 1)
            V.memset(hist[:], 0.0).then_inc(s_dve, 1)
            steps.count += 5
            dve.wait_ge(s_edges, 96)
            dve.wait_ge(s_iota, 4)
            step(V.tensor_scalar(tmp_i, dst_i, 7, None, op0=ALU.arith_shift_right))
            step(V.tensor_copy(key, tmp_i))
            step(V.tensor_scalar(tmp_i, dst_i, P - 1, None, op0=ALU.bitwise_and))
            step(V.scalar_tensor_tensor(out=rec, in0=src_i, scalar=float(R), in1=et_i, op0=ALU.mult, op1=ALU.add))
            step(V.scalar_tensor_tensor(out=rec, in0=tmp_i, scalar=65536.0, in1=rec, op0=ALU.mult, op1=ALU.add))
            step(V.tensor_scalar(val, key, float(NT), INVALID, op0=ALU.is_equal, op1=ALU.mult))
            step(V.tensor_tensor(rec, rec, val, ALU.add))
            with dve.Fori(0, K) as k:
                steps.enter(k, 1)
                step(V.tensor_scalar(onek, key, iota_k[:, ds(k, 1)], 0.0, op0=ALU.is_equal, op1=ALU.add,
                                accum_out=hist[:, ds(k, 1)]))
                steps.leave(K)
            dve.sem_inc(s_hist, 1)
            dve.wait_ge(s_prefill, 16)

            def w_low(dest, high, g, k):
                dve.wait_ge(s_whi, g + k + 1)
                V.scalar_tensor_tensor(out=dest, in0=psH[k][:], scalar=SW, in1=high,
                                       op0=ALU.mult, op1=ALU.subtract).then_inc(s_wlo, 1)

            with dve.Fori(0, R) as r:
                for k in range(KB):
                    w_low(wrel[:, ds(r, 1), k, 1, :].rearrange("p r d -> p (r d)"),
                          wrel[:, ds(r, 1), k, 0, :].rearrange("p r d -> p (r d)"), r * KB, k)
            for k in range(KB):
                w_low(wself[:, k, 1, :], wself[:, k, 0, :], R * KB, k)
            dve.wait_ge(s_tot, 1)
            step(V.tensor_copy(total[:], psM[0][:, 0:K]))
            step(V.tensor_copy(base[:], psM[1][:, 0:K]))
            step(V.tensor_scalar(total_i[:], total[:], float(P - 1), None, op0=ALU.add))
            step(V.tensor_scalar(total_i[:], total_i[:], 7, None, op0=ALU.arith_shift_right))
            step(V.tensor_copy(nchunk[:], total_i[:]))
            step(V.tensor_tensor_scan(cend[:], onesk[:], nchunk[:], 0.0, ALU.mult, ALU.add))
            step(V.tensor_tensor(total[:], cend[:], nchunk[:], ALU.subtract))
            step(V.scalar_tensor_tensor(out=base[:], in0=total[:], scalar=float(P), in1=base[:], op0=ALU.mult, op1=ALU.add))
            step(V.tensor_scalar(base[:], base[:], -1.0, None, op0=ALU.add))

            def x_low(j, t):
                dve.wait_ge(s_xhi, t + 1)
                V.scalar_tensor_tensor(out=xT[:, j, 1, :], in0=psT[j][:], scalar=SX, in1=xT[:, j, 0, :],
                                       op0=ALU.mult, op1=ALU.subtract).then_inc(s_xlo, 1)

            def sort_key(k):
                step(V.tensor_scalar(onek, key, iota_k[:, ds(k, 1)], None, op0=ALU.is_equal))
                step(V.tensor_tensor_scan(cum, onesc, onek, 0.0, ALU.mult, ALU.add))
                step(V.scalar_tensor_tensor(out=val, in0=cum, scalar=base[:, ds(k, 1)], in1=onek, op0=ALU.add, op1=ALU.mult))
                step(V.tensor_tensor(pos, pos, val, ALU.add))
                step(V.scalar_tensor_tensor(out=tiles, in0=cidx, scalar=cend[:, ds(k, 1)], in1=tiles, op0=ALU.is_ge, op1=ALU.add))

            def h_low(j, t, key0=None):
                for r in range(R):
                    dve.wait_ge(s_hhi, R * t + r + 1)
                    V.scalar_tensor_tensor(out=hst[:, j, r, 1, :], in0=psH[r % 4][:], scalar=SH / (SX * SW),
                                           in1=hst[:, j, r, 0, :], op0=ALU.mult, op1=ALU.subtract).then_inc(s_hlo, 1)
                    if key0 is not None and r in (1, 4, 7):
                        sort_key(key0 + (1, 4, 7).index(r))

            PER_PAIR = 2 * KPT * 5
            x_low(0, 0)
            with dve.Fori(0, SORT_PAIRS) as u:
                steps.enter(u, PER_PAIR)
                x_low(1, 2 * u + 1)
                h_low(0, 2 * u, 2 * KPT * u)
                x_low(0, 2 * u + 2)
                h_low(1, 2 * u + 1, 2 * KPT * u + KPT)
                steps.leave(SORT_PAIRS)
            step(V.tensor_copy(pos_i, pos))
            dve.sem_inc(s_pos, 1)
            step(V.tensor_scalar(tiles, tiles, float(NT - 1), None, op0=ALU.min))
            step(V.tensor_copy(tile_i[:], tiles[0:1, :]))
            step(V.memset(same_prev, 0.0))
            step(V.memset(same_next, 0.0))
            step(V.tensor_tensor(same_prev[:, 1:NCP], tiles[:, 1:NCP], tiles[:, 0:NCP - 1], ALU.is_equal))
            step(V.tensor_tensor(same_next[:, 0:NCP - 1], tiles[:, 0:NCP - 1], tiles[:, 1:NCP], ALU.is_equal))
            with dve.Fori(SORT_PAIRS, PAIRS) as u:
                x_low(1, 2 * u + 1)
                h_low(0, 2 * u)
                x_low(0, 2 * u + 2)
                h_low(1, 2 * u + 1)
            h_low(0, NT - 1)

            dve.wait_ge(s_slotT, 1)
            step(V.tensor_copy(rec_i[:, 0:4 * P], psM[0][:, 0:4 * P]))
            step(V.tensor_copy(rec_i[:, 4 * P:NCP], psM[1][:, 0:NCP - 4 * P]))
            step(V.tensor_scalar(gidx[:], rec_i, 65535, None, op0=ALU.bitwise_and))
            step(V.tensor_scalar(t_i, rec_i, 16, None, op0=ALU.arith_shift_right))
            step(V.tensor_copy(rowT[:], t_i))
            step(V.tensor_scalar(t_i, rec_i, R - 1, None, op0=ALU.bitwise_and))
            step(V.tensor_copy(relT, t_i))
            step(V.tensor_tensor(rel1, relT.unsqueeze(2).broadcast_to([P, NCP, R]),
                                 iota_k[:, 0:R].unsqueeze(1).broadcast_to([P, NCP, R]), ALU.is_equal))
            step(V.tensor_copy(slotc_i, slotc))
            step(V.tensor_scalar(slotc_i, slotc_i, 16, None, op0=ALU.arith_shift_right))
            step(V.tensor_copy(rowc, slotc_i))
            dve.sem_inc(s_rowc, 1)
            dve.wait_ge(s_st[0], 16 * (PAIRS + 1))
            dve.wait_ge(s_st[1], 16 * PAIRS)
            step(V.memset(cnt[:, :, NCH:NCP], 0.0))
            with dve.Fori(0, NT) as i:
                for j in range(2):
                    dve.wait_ge(s_cnt, 2 * i + j + 1)
                    c0 = (2 * i + j) * HALF
                    V.tensor_tensor(D1[:, j], rowT[:, ds(c0, HALF)].unsqueeze(2).broadcast_to([P, HALF, P]),
                                    iota_row[:].unsqueeze(1).broadcast_to([P, HALF, P]), ALU.is_equal).then_inc(s_D1, 1)
            dve.wait_ge(s_cntc, 2 + 2 * NT)
            for r in range(R):
                V.tensor_tensor_scan(run[:, r], same_prev, cnt[:, r], 0.0, ALU.mult, ALU.add).then_inc(s_dve, 1)
            steps.count += R - 1
            step(None)
            bc = same_next.unsqueeze(1).broadcast_to([P, R, NCP])
            step(V.tensor_tensor(cnt, run, bc, ALU.mult))
            step(V.tensor_tensor(cnt, run, cnt, ALU.subtract))
            for r in range(R):
                V.tensor_tensor_scan(run[:, r, ::-1], same_next[:, ::-1], cnt[:, r, ::-1], 0.0, ALU.mult, ALU.add).then_inc(s_dve, 1)
            steps.count += R - 1
            step(None)
            step(V.tensor_scalar(run, run, 1.0, None, op0=ALU.max))
            step(V.reciprocal(cnt, run))
            step(V.tensor_scalar(inv[:, 0:R], cnt, SWT, None, op0=ALU.mult))
            step(V.scalar_tensor_tensor(out=inv[:, R:2 * R].rearrange("p r c -> p (r c)"), in0=cnt.rearrange("p r c -> p (r c)"), scalar=SWT,
                                        in1=inv[:, 0:R].rearrange("p r c -> p (r c)"), op0=ALU.mult, op1=ALU.subtract))
            dve.sem_inc(s_inv, 1)
            step(V.memset(wgt[:, NCH:NCP, :], 0.0))
            with dve.Fori(0, NT) as i:
                steps.enter(i, 2)
                for j in range(2):
                    c0 = (2 * i + j) * HALF
                    dve.wait_ge(s_rb[j], 16 * (i + 1))
                    dve.wait_ge(s_look, 2 * i + j + 1)
                    V.tensor_scalar(DT[:, j], rows_b[:, j], iota_part[:, 0:1], None, op0=ALU.is_equal).then_inc(s_DT, 1)
                    dve.wait_ge(s_look, 2 + 2 * i + j + 1)
                    step(V.tensor_tensor(prod, psM[j][:, 0:HALF * 2 * R].rearrange("p (c q r) -> p c q r", q=2, r=R),
                                         rel1[:, ds(c0, HALF), :].unsqueeze(2).broadcast_to([P, HALF, 2, R]), ALU.mult))
                    V.tensor_reduce(wgt[:, ds(c0, HALF), :], prod, op=ALU.add, axis=AX.X).then_inc(s_w8, 1)
                steps.leave(NT)
            dve.wait_ge(s_w8, 2 + 2 * NT)
            dve.wait_ge(s_accz, NT)

            def one_hots(c, b):
                dve.wait_ge(s_mm, c + 1)
                for q in range(2):
                    ins = V.tensor_scalar(onehot[:, b, q, :], iota_row[:], rowT[:, ds(c, 1)],
                                          wgt[:, ds(c, 1), q], op0=ALU.is_equal, op1=ALU.mult)
                ins.then_inc(s_S, 1)

            for s in range(3):
                one_hots(s, s)
            with dve.Fori(0, NT) as i:
                for s in range(CPT):
                    c = CPT * i + s
                    one_hots(c + 3, (s + 3) % 6)
                    t = dve.value_load(tile_i[0:1, ds(c, 1)], min_val=0, max_val=NT - 1)
                    dve.wait_ge(s_mm, 6 + c + 1)
                    dve.wait_ge(s_acc, 3 + c)
                    row = flat(acc[:, ds(t, 1), :])
                    V.scalar_tensor_tensor(out=row, in0=psH[s % 3][:], scalar=1.0 / (SH * SWT), in1=row,
                                           op0=ALU.mult, op1=ALU.add).then_inc(s_acc, 1)
                    if s == 6:
                        dve.wait_ge(s_x2hi, i + 1)
                        V.scalar_tensor_tensor(out=xT[:, 0, 1, :], in0=psT[0][:], scalar=SX, in1=xT[:, 0, 0, :],
                                               op0=ALU.mult, op1=ALU.subtract).then_inc(s_x2lo, 1)
                    if s == 13:
                        dve.wait_ge(s_self, i + 1)
                        dve.wait_ge(s_acc, 3 + c + 1)
                        own = flat(acc[:, ds(i, 1), :])
                        V.scalar_tensor_tensor(out=own, in0=psH[3][:], scalar=1.0 / (SX * SW), in1=own,
                                               op0=ALU.mult, op1=ALU.add).then_inc(s_own, 1)
                        dve.wait_ge(s_own, i + 1)
                        V.tensor_tensor(own, own, xst[:, 0, :], ALU.add).then_inc(s_selfa, 1)
                        dve.wait_ge(s_selfa, 1 + i + 1)
            dve.wait_ge(s_acc, 3 + NCH)
            with dve.Fori(0, NT) as i:
                steps.enter(i, 3)
                V.bn_stats(stats[:, 0, :], flat(acc[:, ds(i, 1), :])).then_inc(s_dve, 1)
                step(None)
                dve.sem_inc(s_stats, 1)
                step(V.bn_aggr(stats[:, 1, 0:2], stats[:, 0, :]))
                step(V.tensor_copy(flat(mv[:, ds(i, 1), :]), stats[:, 1, 0:2]))
                steps.leave(NT)
            step(V.tensor_scalar(mv[:, :, 1], mv[:, :, 1], EPS, None, op0=ALU.add))
            dve.sem_inc(s_mv, 1)
            dve.wait_ge(s_std, 1)
            step(V.reciprocal(mv[:, :, 1], mv[:, :, 1]))
            with dve.Fori(0, NT) as i:
                V.tensor_scalar(flat(acc[:, ds(i, 1), :]), flat(acc[:, ds(i, 1), :]), mv[:, ds(i, 1), 0],
                                mv[:, ds(i, 1), 1], op0=ALU.subtract, op1=ALU.mult).then_inc(s_y, 1)


class Steps:

    def __init__(self, engine, semaphore):
        self.engine, self.semaphore = engine, semaphore
        self.count, self.before = 0, 0

    def step(self, instruction):
        self.count += 1
        if instruction is not None:
            instruction.then_inc(self.semaphore, 1)
        self.engine.wait_ge(self.semaphore, self.before + self.count)

    def enter(self, i, per):
        self.outside, self.per = self.count, per
        self.before = i * per

    def leave(self, turns):
        assert self.count - self.outside == self.per, (self.count, self.outside, self.per)
        self.count = self.outside + turns * self.per
        self.before = 0


def kernel(**inputs):
    import numpy as np
    import concourse.bacc as bacc
    from concourse.bass_utils import run_bass_kernel_spmd

    nc = bacc.Bacc("TRN2", target_bir_lowering=False, num_devices=1)
    arrays, args = {}, []
    for name in ("x", "src", "dst", "edge_type_8", "L0_gnn_W_self", "L0_gnn_W_rel", "L0_gnn_bias"):
        a = np.ascontiguousarray(inputs[name])
        arrays["in_" + name] = a
        args.append(nc.dram_tensor("in_" + name, a.shape, mybir.dt.from_np(a.dtype), kind="ExternalInput").ap())
    out = nc.dram_tensor("out", arrays["in_x"].shape, mybir.dt.float32, kind="ExternalOutput").ap()
    build_gnn(nc, *args, out)
    return run_bass_kernel_spmd(nc, [arrays], core_ids=[0]).results[0]["out"]
```

```python
import concourse.bass as bass
from concourse import mybir
from contextlib import ExitStack


def build_gnn(nc, x, src, dst, etype, w_self, w_rel, bias, out):
    f32, f16, i32 = mybir.dt.float32, mybir.dt.float16, mybir.dt.int32
    ALU, ACT, AX = mybir.AluOpType, mybir.ActivationFunctionType, mybir.AxisListType
    ds = bass.ds

    P = 128
    N, D = x.shape
    R = w_rel.shape[0]
    E = src.shape[0]
    KB = D // P
    NT = -(-N // P)
    LAST = N - (NT - 1) * P
    PAIRS = (NT - 1) // 2
    C = -(-E // P)
    C = -(-C // NT) * NT
    SC = C // NT
    E_LAST = E - (P - 1) * C
    CPT = -(-((E + NT * (P - 1)) // P) // NT)
    HALF = CPT // 2
    STREAM = CPT * NT // 2
    CG = -(-(CPT * NT) // P)
    NCP = CG * P
    GC = 16
    INVALID = float(P << 16)
    EPS = 1e-5
    SX, SW, SH, SWT = 2.0 ** 6, 2.0 ** 10, 2.0 ** 6, 2.0 ** 10
    UNDER_H = R * 2 * D * 2 // (4 * D)
    ACC_SPLIT = 2 * UNDER_H + (NT - 2 * UNDER_H) // 4 * 2
    NORM = NT // 2
    BANKS = 6

    HIST_END = 3
    KPT = 9
    K = HIST_END * 2 * KPT
    COUNT = 6
    SCAN = COUNT + NCP // GC // 8
    LOOK = SCAN + R // 2
    assert E_LAST > 0 and 2 * PAIRS + 1 == NT and NORM % 4 == 0 and (NT - NORM) % 4 == 1 and CPT % BANKS == 0 and CPT % 2 == 0
    assert K > NT and LOOK + NCP // GC // 8 <= PAIRS and NCP % (8 * GC) == 0

    h = nc.dram_tensor("h_parts", [N * R, 2 * D], f16, kind="Internal").ap()
    h_rows = h.rearrange("(n r) d -> n (r d)", r=R)
    records = nc.dram_tensor("records", [C * P + P, 1], f32, kind="Internal").ap()
    rowids = nc.dram_tensor("sorted_rows", [NCP * P], f16, kind="Internal").ap()

    ctx = ExitStack()
    with ctx:
        def sb(name, shape, dt):
            return ctx.enter_context(nc.sbuf_tensor(name, shape, dt))

        def sem(name):
            return ctx.enter_context(nc.semaphore(name))

        wrel = sb("wrel", [P, R, KB, 2, D], f16)
        wself = sb("wself", [P, KB, 2, D], f16)
        xst = sb("xst", [P, 2, D], f32)
        xT = sb("xT", [P, 2, 2, KB * P], f16)
        arena = sb("arena", [P, (NT + 1) * D], f32)
        gidx = sb("gidx", [P, CPT * NT + HALF], i32)
        rowT = sb("rowT", [P, NCP], f16)
        wgt = sb("wgt", [P, NCP, 2], f32)
        onehot = sb("onehot", [P, BANKS, 2, P], f16)
        rowP = sb("rowP", [P, CPT * NT + HALF], f16)
        tile_i = sb("tile_i", [1, CPT * NT], i32)
        shared_i = sb("shared_i", [1, 1], i32)
        gap = sb("gap", [1, 1], f32)
        ident = sb("ident", [P, P], f32)
        before = sb("before", [P, P], f32)
        ones = sb("ones", [P, P], f32)
        iota_row = sb("iota_row", [P, P], f16)
        iota_part = sb("iota_part", [P, 1], f32)
        iota_k = sb("iota_k", [P, K], f32)
        chunk_of = sb("chunk_of", [P, CG], f32)
        idx_a = sb("idx_a", [P, max(SC, CPT)], i32)
        rec_a = sb("rec_a", [P, SC], f32)
        padrec = sb("padrec", [1, P], f32)
        biasb = sb("biasb", [P, D], f32)
        hist = sb("hist", [P, K], f32)
        total = sb("total", [P, K], f32)
        total_i = sb("total_i", [P, K], i32)
        nchunk = sb("nchunk", [P, K], f32)
        cend = sb("cend", [P, K], f32)
        eend = sb("eend", [P, K], f32)
        lag = sb("lag", [P, K], f32)
        base = sb("base", [P, K], f32)
        onesk = sb("onesk", [P, K], f32)
        unsorted = sb("unsorted", [P, 1], f32)
        unsorted_i = sb("unsorted_i", [1, 1], i32)
        ctile = sb("ctile", [P, CG], f32)
        estart = sb("estart", [P, CG], f32)
        estart_i = sb("estart_i", [P, CG], i32)
        nvalid = sb("nvalid", [P, CG], f32)

        acc = arena[:, :].rearrange("p (t d) -> p t d", d=D)
        used = [0]

        def view(n, dt, at=None):
            size = {f32: 4, i32: 4, f16: 2}[dt] * n
            start = used[0] if at is None else at
            used[0] = start + size
            assert start % 4 == 0 and size % 4 == 0 and used[0] <= (NT + 1) * D * 4, (start, size)
            v = arena[:, start // 4:(start + size) // 4]
            return v if dt == f32 else v.bitcast(dt)

        hst = view(2 * R * 2 * D, f16).rearrange("p (j r c d) -> p j r c d", j=2, r=R, c=2)
        counts_at = used[0]
        cnt = view(R * NCP, f32).rearrange("p (r c) -> p r c", r=R)
        inv = view(R * 2 * NCP, f16, at=counts_at).rearrange("p (r q c) -> p r q c", r=R, q=2)
        rel1 = view(NCP * R, f16).rearrange("p (c r) -> p c r", r=R)
        dbuf_at = used[0]
        D1 = view(2 * GC * P, f16).rearrange("p (j c d) -> p j c d", j=2, c=GC)
        rows_b = view(2 * GC * P, f16).rearrange("p (j c d) -> p j c d", j=2, c=GC)
        same_prev = view(NCP, f16)
        same_next = view(NCP, f16)
        run = view(NCP, f32)
        relg = view(2 * GC * R, f16).rearrange("p (j c r) -> p j c r", j=2, r=R)
        invg = view(2 * GC * 2 * R, f16).rearrange("p (j c q) -> p j c q", j=2, q=2 * R)
        prod = view(GC * 2 * R, f32).rearrange("p (c r q) -> p c r q", q=2, r=R)
        wst = view(2 * KB * D, f32, at=0).rearrange("p (j b i) -> p j b i", j=2, b=KB)
        even = -(-(C + 1) // 2) * 2
        key = view(even, f16, at=counts_at)[:, 0:C + 1]
        onek = view(even, f16)[:, 0:C]
        cum = view(even, f16)[:, 0:C]
        onesc = view(even, f16)[:, 0:C]
        pos = view(C, f32)
        rec = view(C, f32)
        val = view(C, f32)
        dst_i = view(C + 1, i32)
        src_i = view(C, i32)
        et_i = view(C, i32)
        tmp_i = view(C + 1, i32)
        pos_i = view(C, i32)
        assert used[0] <= dbuf_at
        slotc = view(NCP, f32, at=dbuf_at)
        slotc_i = view(NCP, i32)
        rowc = view(NCP, f16)
        rec_at = used[0]
        rec_i = view(NCP, i32)
        relT = view(NCP, f32)
        diag = view(NCP, f32, at=rec_at).rearrange("p (g e) -> p g e", g=CG)
        tmpc = view(NCP, f32, at=dbuf_at)
        cmp = view(2 * CG * NT, f32, at=dbuf_at).rearrange("p (a g k) -> p a g k", a=2, g=CG)
        gath = wrel[:, 0:5].rearrange("p r k a d -> p (r k a d)")[:, 0:CPT * 2 * D].rearrange(
            "p (b q d) -> p b q d", b=CPT, q=2)
        dgrp = wrel[:, 5].rearrange("p k a d -> p (k a d)")[:, 0:2 * HALF * P].rearrange(
            "p (j c d) -> p j c d", j=2, c=HALF)
        stat = wrel[:, 7].rearrange("p k a d -> p (k a d)").bitcast(f32)
        stats = stat[:, 0:6 * NT].rearrange("p (t s) -> p t s", s=6)
        mean, var, rstd, nbias = (stat[:, (6 + n) * NT:(7 + n) * NT] for n in range(4))

        psT = [ctx.enter_context(nc.psum_tensor(f"psT{j}", [P, D], f32)) for j in range(2)]
        psH = [ctx.enter_context(nc.psum_tensor(f"psH{j}", [P, D], f32)) for j in range(4)]
        psM = [ctx.enter_context(nc.psum_tensor(f"psM{j}", [P, D], f32)) for j in range(2)]
        ps2 = psH + psM

        s_const = sem("consts_made")
        s_clear = sem("matrices_cleared")
        s_iota = sem("iotas_made")
        s_edges = sem("edges_loaded")
        s_blank = sem("edge_buffers_padded")
        s_bias = sem("bias_loaded")
        s_w = [sem(f"w_loaded{j}") for j in range(2)]
        s_wT = sem("w_transposed")
        s_whi = sem("w_high_made")
        s_wlo = sem("w_low_made")
        s_dve = sem("dve_step")
        s_dveu = sem("dve_sort_step")
        s_x = [sem(f"x_loaded{j}") for j in range(2)]
        s_xT = sem("x_transposed")
        s_xhi = sem("x_high_made")
        s_xlo = sem("x_low_made")
        s_h = sem("h_summed")
        s_hhi = sem("h_high_made")
        s_hlo = sem("h_low_made")
        s_st = [sem(f"h_stored{j}") for j in range(2)]
        s_rec = sem("records_made")
        s_recst = sem("records_stored")
        s_hist = sem("histogram_made")
        s_tot = sem("totals_summed")
        s_tab = sem("chunk_tables_made")
        s_tiles = sem("chunk_tiles_broadcast")
        s_pos = sem("positions_ready")
        s_stage = sem("scatter_staged")
        s_sc = [sem(f"scattered{j}") for j in range(SC)]
        s_slotg = sem("slots_gathered")
        s_rowc = sem("slots_masked")
        s_slotT = sem("slots_transposed")
        s_rowst = sem("rowids_stored")
        s_folded = sem("identity_added")
        s_D1 = sem("count_operands_made")
        s_cnt = sem("group_counted")
        s_cntc = sem("counts_copied")
        s_inv = sem("inverses_made")
        s_rb = [sem(f"rows_broadcast{j}") for j in range(2)]
        s_invg = sem("group_inverses_copied")
        s_DT = sem("transposed_one_hots_made")
        s_look = sem("group_looked_up")
        s_w8 = sem("weights_made")
        s_go = sem("pool_waits_passed")
        s_accz = sem("acc_initialised")
        s_idx = sem("indices_staged")
        s_g = [sem(f"gathered{b}") for b in range(CPT)]
        s_D = sem("edge_one_hots_made")
        s_S = sem("edge_weights_placed")
        s_mm = sem("chunk_summed")
        s_acc = sem("chunk_added")
        s_x2 = sem("x_reloaded")
        s_x2T = sem("x2_transposed")
        s_x2hi = sem("x2_high_made")
        s_x2lo = sem("x2_low_made")
        s_self = sem("self_summed")
        s_merged = sem("spare_added")
        s_selfa = sem("self_added")
        s_mv = sem("moments_made")
        s_std = sem("deviation_made")
        s_rstd = sem("scales_made")
        s_y = [sem(f"normalised{j}") for j in range(2)]
        s_out = sem("out_stored")

        block = ctx.enter_context(nc.Block())

        def flat(t):
            return t.rearrange("p a b -> p (a b)")

        @block.sync
        def _(sp):
            sp.dma_start(wst[:, 0], w_rel[0].rearrange("(b p) i -> p b i", p=P)).then_inc(s_w[0], 16)
            sp.dma_start(wst[:, 1], w_rel[1].rearrange("(b p) i -> p b i", p=P)).then_inc(s_w[1], 16)
            sp.dma_start(xst[:, 0], x[0:P, :]).then_inc(s_x[0], 16)
            sp.dma_start(xst[:, 1], x[P:2 * P, :]).then_inc(s_x[1], 16)
            with sp.Fori(1, R // 2) as u:
                for j in range(2):
                    sp.wait_ge(s_wT, KB * (2 * u + j - 1))
                    sp.dma_start(wst[:, j], w_rel[ds(2 * u + j, 1)].rearrange("r (b p) i -> p (r b) i", p=P)).then_inc(s_w[j], 16)
            sp.wait_ge(s_wT, KB * (R - 1))
            sp.dma_start(wst[:, 0], w_self.rearrange("(b p) i -> p b i", p=P)).then_inc(s_w[0], 16)
            sp.wait_ge(s_blank, 1)
            sp.dma_start(dst_i[0:P - 1, :], bass.AP(tensor=dst.tensor, offset=dst.offset, ap=[[C, P - 1], [1, C + 1]])).then_inc(s_edges, 16)
            sp.dma_start(dst_i[P - 1:P, 0:E_LAST], dst[(P - 1) * C:E].rearrange("(p c) -> p c", p=1)).then_inc(s_edges, 16)
            for arr, buf in ((src, src_i), (etype, et_i)):
                sp.dma_start(buf[0:P - 1, :], arr[0:(P - 1) * C].rearrange("(p c) -> p c", c=C)).then_inc(s_edges, 16)
                sp.dma_start(buf[P - 1:P, 0:E_LAST], arr[(P - 1) * C:E].rearrange("(p c) -> p c", p=1)).then_inc(s_edges, 16)
            sp.dma_start(biasb[:], bias.rearrange("(o d) -> o d", o=1).broadcast_to([P, D])).then_inc(s_bias, 16)

            def store_h(t, j, n=P):
                sp.wait_ge(s_hlo, 4 + R * (t + 1))
                sp.dma_start(h_rows[ds(t * P, n), :],
                             hst[0:n, j].rearrange("p r c d -> p (r c d)")).then_inc(s_st[j], 16)

            with sp.Fori(0, PAIRS - 1) as u:
                for j in range(2):
                    t = 2 * u + j
                    sp.wait_ge(s_xT, t + 1)
                    sp.dma_start(xst[:, j], x[ds((t + 2) * P, P), :]).then_inc(s_x[j], 16)
                    store_h(t, j)
            sp.wait_ge(s_xT, NT - 2)
            sp.dma_start(xst[0:LAST, 0], x[(NT - 1) * P:N, :]).then_inc(s_x[0], 16)
            store_h(NT - 3, 0)
            store_h(NT - 2, 1)
            store_h(NT - 1, 0, LAST)
            with sp.Fori(0, NT - 1) as i:
                sp.wait_ge(s_x2lo, i + 1)
                sp.dma_start(xst[:, 0], x[ds(i * P, P), :]).then_inc(s_x2, 16)
            sp.wait_ge(s_x2lo, NT)
            sp.dma_start(xst[0:LAST, 0], x[(NT - 1) * P:N, :]).then_inc(s_x2, 16)
            with sp.Fori(0, NORM) as i:
                sp.wait_ge(s_y[1], i + 1)
                sp.dma_start(out[ds(i * P, P), :], flat(acc[:, ds(i, 1), :])).then_inc(s_out, 16)
            with sp.Fori(0, (NT - NORM) // 2) as i:
                for j in range(2):
                    t = NORM + 2 * i + j
                    sp.wait_ge(s_y[j], i + 1 + NORM * j)
                    sp.dma_start(out[ds(t * P, P), :], flat(acc[:, ds(t, 1), :])).then_inc(s_out, 16)
            sp.wait_ge(s_y[0], (NT - NORM) // 2 + 1)
            sp.dma_start(out[(NT - 1) * P:N, :], acc[0:LAST, NT - 1, :]).then_inc(s_out, 16)
            sp.wait_ge(s_out, 16 * NT)

        @block.tensor
        def _(pe):
            pe.wait_ge(s_const, 6)

            def w_transposes(j, n_w, g):
                pe.wait_ge(s_w[j], 16 * n_w)
                for k in range(KB):
                    pe.wait_ge(s_wlo, g + k + 1)
                    for b in range(KB):
                        last = nc.tensor.transpose(psH[k][:, b * P:(b + 1) * P], wst[:, j, b, k * P:(k + 1) * P], ident[:])
                    last.then_inc(s_wT, 1)

            with pe.Fori(0, R // 2) as u:
                for j in range(2):
                    w_transposes(j, u + 1, (2 * u + j) * KB)
            pe.wait_ge(s_folded, KB)
            w_transposes(0, R // 2 + 1, R * KB)

            def x_transposes(j, n_x, t):
                pe.wait_ge(s_x[j], 16 * n_x)
                pe.wait_ge(s_xlo, t + 1)
                for k in range(KB):
                    last = nc.tensor.transpose(psT[j][:, k * P:(k + 1) * P], xst[:, j, k * P:(k + 1) * P], ident[:])
                last.then_inc(s_xT, 1)

            def products(bank, j, w):
                for k in range(KB):
                    hi, lo = xT[:, j, 0, k * P:(k + 1) * P], xT[:, j, 1, k * P:(k + 1) * P]
                    nc.tensor.matmul(bank[:], hi, w[:, k, 0, :], start=(k == 0), stop=False)
                    nc.tensor.matmul(bank[:], hi, w[:, k, 1, :], start=False, stop=False)
                    last = nc.tensor.matmul(bank[:], lo, w[:, k, 0, :], start=False, stop=(k == KB - 1))
                return last

            def tile_products(j, t, group=None, g0=0):
                pe.wait_ge(s_xlo, 2 + t + 1)
                for r in range(R):
                    pe.wait_ge(s_hlo, R * t + r + 1)
                    products(psH[r % 4], j, wrel[:, r]).then_inc(s_h, 1)
                    if group and r % 2:
                        group(g0 + r // 2, r // 2 % 2)

            def pair(u, mid=None, group=None, g0=0):
                x_transposes(1, u + 1, 2 * u + 1)
                tile_products(0, 2 * u, group, g0)
                x_transposes(0, u + 2, 2 * u + 2)
                if mid:
                    mid()
                tile_products(1, 2 * u + 1, group, g0 + 4)

            def totals():
                pe.wait_ge(s_hist, 1)
                nc.tensor.matmul(psM[0][:, 0:K], ones[:], hist[:], start=True, stop=True)
                nc.tensor.matmul(psM[0][:, K:K + 1], ones[:], unsorted[:], start=True, stop=True)
                nc.tensor.matmul(psM[1][:, 0:K], before[:], hist[:], start=True, stop=True).then_inc(s_tot, 1)

            def chunk_tiles():
                pe.wait_ge(s_tab, 1)
                for g in range(CG):
                    last = nc.tensor.matmul(psM[g // 4][:, (g % 4) * P:(g % 4 + 1) * P], ones[:], diag[:, g, :],
                                            start=True, stop=True)
                last.then_inc(s_tiles, 1)

            def slot_transposes():
                pe.wait_ge(s_rowc, 1)
                for g in range(CG):
                    last = nc.tensor.transpose(psM[g // 4][:, (g % 4) * P:(g % 4 + 1) * P], slotc[:, g * P:(g + 1) * P], ident[:])
                last.then_inc(s_slotT, 1)

            def count(g, j):
                pe.wait_ge(s_D1, 2 * g + 2)
                pe.wait_ge(s_cntc, g + 1)
                for c in range(GC):
                    last = nc.tensor.matmul(psM[j][:, c * R:(c + 1) * R], D1[:, j, c, :],
                                            relg[:, j, c, :], start=True, stop=True)
                last.then_inc(s_cnt, 1)

            def look_up(g, j):
                pe.wait_ge(s_DT, 2 + g + 1)
                pe.wait_ge(s_invg, g + 1)
                pe.wait_ge(s_w8, g + 1)
                for c in range(GC):
                    last = nc.tensor.matmul(psM[j][:, c * 2 * R:(c + 1) * 2 * R], D1[:, j, c, :],
                                            invg[:, j, c, :], start=True, stop=True)
                last.then_inc(s_look, 1)

            pe.wait_ge(s_wlo, KB + KB * (R + 1))
            x_transposes(0, 1, 0)
            with pe.Fori(0, HIST_END) as u:
                pair(u)
            pair(HIST_END, mid=totals)
            pair(HIST_END + 1, mid=chunk_tiles)
            pair(HIST_END + 2, mid=slot_transposes)
            with pe.Fori(COUNT, SCAN) as u:
                pair(u, group=count, g0=8 * (u - COUNT))
            with pe.Fori(SCAN, LOOK) as u:
                pair(u)
            pe.wait_ge(s_inv, 1)
            with pe.Fori(LOOK, PAIRS) as u:
                pair(u, group=look_up, g0=8 * (u - LOOK))
            tile_products(0, NT - 1)

            pe.sem_inc(s_mm, BANKS)
            with pe.Fori(0, NT) as i:
                for s in range(CPT):
                    c = CPT * i + s
                    if s == 5:
                        pe.wait_ge(s_x2, 16 * (i + 1))
                        pe.wait_ge(s_x2lo, i + 1)
                        for k in range(KB):
                            last = nc.tensor.transpose(psT[0][:, k * P:(k + 1) * P], xst[:, 0, k * P:(k + 1) * P], ident[:])
                        last.then_inc(s_x2T, 1)
                    b = s % BANKS
                    pe.wait_ge(s_S, HALF + c + 1)
                    pe.wait_ge(s_acc, c + 1)
                    pe.wait_ge(s_g[s], 16 * (i + 1))
                    bank = ps2[b]
                    nc.tensor.matmul(bank[:], onehot[:, b, 0, :], gath[:, s, 0, :], start=True, stop=False)
                    nc.tensor.matmul(bank[:], onehot[:, b, 0, :], gath[:, s, 1, :], start=False, stop=False)
                    nc.tensor.matmul(bank[:], onehot[:, b, 1, :], gath[:, s, 0, :], start=False, stop=True).then_inc(s_mm, 1)
                    if s == 12:
                        pe.wait_ge(s_x2lo, i + 2)
                        pe.wait_ge(s_selfa, i + 1)
                        products(psT[1], 0, wself).then_inc(s_self, 1)

        @block.scalar
        def _(act):
            act.sem_inc(s_cntc, 2)

            def w_high(dest, g, k):
                act.wait_ge(s_wT, g + k + 1)
                nc.scalar.activation(dest, psH[k][:], ACT.Copy, scale=SW).then_inc(s_whi, 1)

            with act.Fori(0, R) as r:
                for k in range(KB):
                    w_high(wrel[:, ds(r, 1), k, 0, :].rearrange("p r d -> p (r d)"), r * KB, k)
            for k in range(KB):
                w_high(wself[:, k, 0, :], R * KB, k)

            def x_high(j, t, reused=True):
                act.wait_ge(s_xT, t + 1)
                if reused:
                    act.wait_ge(s_h, R * (t - 1))
                nc.scalar.activation(xT[:, j, 0, :], psT[j][:], ACT.Copy, scale=SX).then_inc(s_xhi, 1)

            def h_high(j, t, reused=True, group=None, g0=0):
                for r in range(R):
                    act.wait_ge(s_h, R * t + r + 1)
                    if r == 0 and reused:
                        act.wait_ge(s_st[j], 8 * (t - j))
                    nc.scalar.activation(hst[:, j, r, 0, :], psH[r % 4][:], ACT.Copy,
                                         scale=SH / (SX * SW)).then_inc(s_hhi, 1)
                    if group and r % 2:
                        group(g0 + r // 2, r // 2 % 2)

            def copy_counts(g, j):
                act.wait_ge(s_cnt, 2 + g + 1)
                nc.scalar.activation(cnt[:, :, ds(g * GC, GC)],
                                     psM[j][:, 0:GC * R].rearrange("p (c r) -> p r c", r=R), ACT.Copy).then_inc(s_cntc, 1)

            def pair(u, **kw):
                g0 = kw.pop("g0", 0)
                x_high(0, 2 * u + 2)
                h_high(1, 2 * u + 1, g0=g0, **kw)
                x_high(1, 2 * u + 3)
                h_high(0, 2 * u + 2, g0=g0 + 4, **kw)

            x_high(0, 0, reused=False)
            act.wait_ge(s_wlo, KB + KB * (R + 1))
            x_high(1, 1, reused=False)
            h_high(0, 0, reused=False)
            x_high(0, 2)
            h_high(1, 1, reused=False)
            x_high(1, 3)
            h_high(0, 2)
            with act.Fori(1, COUNT - 1) as u:
                pair(u)
            x_high(0, 2 * COUNT)
            h_high(1, 2 * COUNT - 1)
            x_high(1, 2 * COUNT + 1)
            h_high(0, 2 * COUNT, group=copy_counts, g0=0)
            with act.Fori(COUNT, SCAN - 1) as u:
                pair(u, group=copy_counts, g0=8 * (u - COUNT) + 4)
            x_high(0, 2 * SCAN)
            h_high(1, 2 * SCAN - 1, group=copy_counts, g0=8 * (SCAN - COUNT) - 4)
            x_high(1, 2 * SCAN + 1)
            h_high(0, 2 * SCAN)
            with act.Fori(SCAN, PAIRS - 1) as u:
                pair(u)
            x_high(0, NT - 1)
            h_high(1, NT - 2)
            act.wait_ge(s_bias, 16)
            act.wait_ge(s_w8, 2 + NCP // GC)
            with act.Fori(ACC_SPLIT, NT) as i:
                nc.scalar.activation(flat(acc[:, ds(i, 1), :]), biasb[:], ACT.Copy).then_inc(s_accz, 1)
            h_high(0, NT - 1)
            nc.scalar.activation(idx_a[:, 0:HALF], gidx[:, 0:HALF], ACT.Copy).then_inc(s_idx, 1)
            act.wait_ge(s_st[1], 16 * PAIRS)
            for t in range(UNDER_H, 2 * UNDER_H):
                nc.scalar.activation(acc[:, t, :], biasb[:], ACT.Copy).then_inc(s_accz, 1)
            act.wait_ge(s_st[0], 16 * (PAIRS + 1))
            for t in range(UNDER_H // 2, UNDER_H):
                nc.scalar.activation(acc[:, t, :], biasb[:], ACT.Copy).then_inc(s_accz, 1)

            with act.Fori(0, NT) as i:
                for s in range(CPT):
                    c = CPT * i + s
                    if s % HALF == 0:
                        act.wait_ge(s_D, 2 * i + s // HALF + 1)
                    sorted_c = HALF * i + s // 2 + s % 2 * STREAM
                    act.wait_ge(s_mm, c + 1)
                    for q in range(2):
                        ins = nc.scalar.activation(onehot[:, s % BANKS, q, :], dgrp[:, s // HALF, s % HALF, :],
                                                   ACT.Copy, scale=wgt[:, ds(sorted_c, 1), q])
                    ins.then_inc(s_S, 1)
                    if s == BANKS - 1:
                        nc.scalar.activation(idx_a[:, HALF:CPT], gidx[:, ds(c - s + HALF, HALF)], ACT.Copy).then_inc(s_idx, 1)
                    if s == HALF + BANKS - 1:
                        nc.scalar.activation(idx_a[:, 0:HALF], gidx[:, ds(c - s + CPT, HALF)], ACT.Copy).then_inc(s_idx, 1)
                    if s == 7:
                        act.wait_ge(s_x2T, i + 1)
                        act.wait_ge(s_selfa, i + 1)
                        nc.scalar.activation(xT[:, 0, 0, :], psT[0][:], ACT.Copy, scale=SX).then_inc(s_x2hi, 1)

            def normalise(t):
                row = flat(acc[:, ds(t, 1), :])
                nc.scalar.activation(row, row, ACT.Identity, bias=nbias[:, ds(t, 1)], scale=rstd[:, ds(t, 1)]).then_inc(s_y[1], 1)

            def deviation(k, lo, hi):
                act.wait_ge(s_mv, k)
                nc.scalar.activation(rstd[:, lo:hi], var[:, lo:hi], ACT.Sqrt).then_inc(s_std, 1)
                act.wait_ge(s_rstd, k)

            deviation(1, 0, NORM)
            with act.Fori(0, NORM // 4) as i:
                for j in range(4):
                    normalise(4 * i + j)
            deviation(2, NORM, NT)
            with act.Fori(0, (NT - NORM) // 4) as i:
                for j in range(2):
                    normalise(NORM + 4 * i + 2 * j + 1)

        @block.gpsimd
        def _(pool):
            nc.gpsimd.memset(ident[:], 0.0).then_inc(s_clear, 1)
            nc.gpsimd.memset(before[:], 0.0).then_inc(s_clear, 1)
            pool.wait_ge(s_clear, 2)
            nc.gpsimd.affine_select(out=ident[:], in_=ident[:], compare_op=ALU.not_equal, fill=1.0, base=0,
                                    pattern=[[-1, P]], channel_multiplier=1).then_inc(s_const, 1)
            nc.gpsimd.affine_select(out=before[:], in_=before[:], compare_op=ALU.is_ge, fill=1.0, base=0,
                                    pattern=[[-1, P]], channel_multiplier=1).then_inc(s_const, 1)
            nc.gpsimd.memset(ones[:], 1.0).then_inc(s_const, 1)
            nc.gpsimd.memset(dst_i, NT * P).then_inc(s_const, 1)
            nc.gpsimd.memset(src_i, 0).then_inc(s_const, 1)
            nc.gpsimd.memset(et_i, 0).then_inc(s_const, 1)
            pool.wait_ge(s_const, 6)
            pool.sem_inc(s_blank, 1)
            nc.gpsimd.iota(iota_row[:], pattern=[[1, P]], base=0, channel_multiplier=0,
                           allow_small_or_imprecise_dtypes=True).then_inc(s_iota, 1)
            nc.gpsimd.iota(iota_part[:], pattern=[[0, 1]], base=0, channel_multiplier=1,
                           allow_small_or_imprecise_dtypes=True).then_inc(s_iota, 1)
            nc.gpsimd.iota(iota_k[:], pattern=[[1, K]], base=0, channel_multiplier=0,
                           allow_small_or_imprecise_dtypes=True).then_inc(s_iota, 1)
            nc.gpsimd.iota(chunk_of[:], pattern=[[P, CG]], base=0, channel_multiplier=1,
                           allow_small_or_imprecise_dtypes=True).then_inc(s_iota, 1)
            nc.gpsimd.memset(padrec[:], INVALID).then_inc(s_iota, 1)
            pool.wait_ge(s_rec, 1)
            pool.wait_ge(s_iota, 5)
            pool.dma_start(records[0:C * P, :].rearrange("(p c) o -> p (c o)", p=P), rec).then_inc(s_recst, 16)
            pool.dma_start(records[C * P:C * P + P, :].rearrange("(o e) i -> o (e i)", o=1), padrec[:]).then_inc(s_recst, 16)
            pool.wait_ge(s_recst, 32)
            pool.wait_ge(s_tab, 1)
            is_unsorted = pool.value_load(unsorted_i[0:1, 0:1], min_val=0, max_val=P)
            with pool.If(is_unsorted > 0):
                pool.wait_ge(s_pos, 1)

                def scatter(i, first=False):
                    for c in range(0 if first else SC):
                        pool.wait_ge(s_sc[c], i * 16)
                    nc.gpsimd.tensor_copy(idx_a[:, 0:SC], pos_i[:, ds(i * SC, SC)]).then_inc(s_stage, 1)
                    nc.gpsimd.tensor_copy(rec_a[:], rec[:, ds(i * SC, SC)]).then_inc(s_stage, 1)
                    pool.wait_ge(s_stage, 2 * i + 2)
                    pool.sem_inc(s_go, 1)
                    for c in range(SC):
                        nc.gpsimd.indirect_dma_start(
                            out=records[:, :], out_offset=bass.IndirectOffsetOnAxis(ap=idx_a[:, c:c + 1], axis=0),
                            in_=rec_a[:, c:c + 1], in_offset=None).then_inc(s_sc[c], 16)

                scatter(0, first=True)
                with pool.Fori(1, NT) as i:
                    scatter(i)
                for c in range(SC):
                    pool.wait_ge(s_sc[c], 16 * NT)
                pool.sem_inc(s_go, 1)
            with pool.Else():
                pool.sem_inc(s_go, 1)
            for g in range(CG):
                nc.gpsimd.indirect_dma_start(
                    out=slotc[:, g * P:(g + 1) * P], out_offset=None, in_=records[:, :],
                    in_offset=bass.IndirectOffsetOnAxis(ap=estart_i[:, g:g + 1], axis=0)).then_inc(s_slotg, 16)
            pool.wait_ge(s_rowc, 1)
            pool.dma_start(rowids.rearrange("(g p e) -> p g e", p=P, e=P),
                           rowc.rearrange("p (g e) -> p g e", g=CG)).then_inc(s_rowst, 16)
            pool.wait_ge(s_rowst, 16)
            pool.wait_ge(s_inv, 1)
            with pool.Fori(0, NCP // GC // 2) as i:
                for j in range(2):
                    pool.wait_ge(s_DT, 2 * i + j + 1)
                    pool.sem_inc(s_go, 1)
                    pool.dma_start(rows_b[:, j].rearrange("p c d -> p (c d)"),
                                   rowids[ds((2 * i + j) * (GC * P), GC * P)].rearrange("(o e) -> o e", o=1)
                                   .broadcast_to([P, GC * P])).then_inc(s_rb[j], 16)
                    pool.wait_ge(s_look, 2 * i + j + 1)
                    nc.gpsimd.tensor_copy(invg[:, j].rearrange("p c q -> p q c"),
                                          inv[:, :, :, ds((2 * i + j) * GC, GC)].rearrange("p r q c -> p (r q) c")
                                          ).then_inc(s_invg, 1)
            pool.wait_ge(s_st[0], 16 * (PAIRS + 1))
            pool.wait_ge(s_st[1], 16 * PAIRS)
            pool.wait_ge(s_w8, 2 + NCP // GC)

            def gathers(i):
                for a in range(2):
                    pool.wait_ge(s_idx, 2 * i + a + 1)
                    pool.sem_inc(s_go, 1)
                    for s in range(a * HALF, (a + 1) * HALF):
                        nc.gpsimd.indirect_dma_start(
                            out=gath[:, s].rearrange("p q d -> p (q d)"), out_offset=None, in_=h[:, :],
                            in_offset=bass.IndirectOffsetOnAxis(ap=idx_a[:, s:s + 1], axis=0)).then_inc(s_g[s], 16)

            with pool.Fori(0, NT) as i:
                gathers(i)

        @block.vector
        def _(dve):
            steps = Steps(dve, s_dve)
            step = steps.step
            V = nc.vector
            dve.sem_inc(s_wlo, KB)
            dve.sem_inc(s_xlo, 2)
            dve.sem_inc(s_hlo, 4)
            dve.sem_inc(s_cnt, 2)
            dve.sem_inc(s_DT, 2)
            dve.sem_inc(s_look, 2)
            dve.sem_inc(s_w8, 2)
            dve.sem_inc(s_S, HALF)
            dve.sem_inc(s_acc, BANKS)
            dve.sem_inc(s_x2lo, 1)
            dve.sem_inc(s_selfa, 1)
            for made in (V.memset(onesc, 1.0), V.memset(onesk[:], 1.0), V.memset(pos, 0.0)):
                made.then_inc(s_dve, 1)
            steps.count += 3

            def w_low(dest, high, g, k):
                dve.wait_ge(s_whi, g + k + 1)
                V.scalar_tensor_tensor(out=dest, in0=psH[k][:], scalar=SW, in1=high,
                                       op0=ALU.mult, op1=ALU.subtract).then_inc(s_wlo, 1)

            with dve.Fori(0, R) as r:
                for k in range(KB):
                    w_low(wrel[:, ds(r, 1), k, 1, :].rearrange("p r d -> p (r d)"),
                          wrel[:, ds(r, 1), k, 0, :].rearrange("p r d -> p (r d)"), r * KB, k)
            dve.wait_ge(s_const, 3)
            dve.wait_ge(s_w[0], 16 * (R // 2 + 1))
            for b in range(KB):
                block_b = wst[:, 0, b, b * P:(b + 1) * P]
                V.tensor_tensor(block_b, block_b, ident[:], ALU.add).then_inc(s_folded, 1)
            for k in range(KB):
                w_low(wself[:, k, 1, :], wself[:, k, 0, :], R * KB, k)

            def x_low(j, t):
                dve.wait_ge(s_xhi, t + 1)
                V.scalar_tensor_tensor(out=xT[:, j, 1, :], in0=psT[j][:], scalar=SX, in1=xT[:, j, 0, :],
                                       op0=ALU.mult, op1=ALU.subtract).then_inc(s_xlo, 1)

            def h_low(j, t, after=None, before=None):
                for r in range(R):
                    if before:
                        before(r)
                    dve.wait_ge(s_hhi, R * t + r + 1)
                    V.scalar_tensor_tensor(out=hst[:, j, r, 1, :], in0=psH[r % 4][:], scalar=SH / (SX * SW),
                                           in1=hst[:, j, r, 0, :], op0=ALU.mult, op1=ALU.subtract).then_inc(s_hlo, 1)
                    if after:
                        after(r)

            def pair(u, after=None, before=None):
                x_low(1, 2 * u + 1)
                h_low(0, 2 * u, after and (lambda r: after(0, r)), before and (lambda r: before(0, r)))
                x_low(0, 2 * u + 2)
                h_low(1, 2 * u + 1, after and (lambda r: after(1, r)), before and (lambda r: before(1, r)))

            x_low(0, 0)
            dve.wait_ge(s_edges, 96)
            dve.wait_ge(s_iota, 4)
            step(V.tensor_scalar(tmp_i, dst_i, 7, None, op0=ALU.arith_shift_right))
            step(V.tensor_copy(key, tmp_i))
            step(V.tensor_scalar(tmp_i, dst_i, P - 1, None, op0=ALU.bitwise_and))
            step(V.scalar_tensor_tensor(out=rec, in0=src_i, scalar=float(R), in1=et_i, op0=ALU.mult, op1=ALU.add))
            step(V.scalar_tensor_tensor(out=rec, in0=tmp_i[:, 0:C], scalar=65536.0, in1=rec, op0=ALU.mult, op1=ALU.add))
            step(V.tensor_scalar(val, key[:, 0:C], float(NT), INVALID, op0=ALU.is_equal, op1=ALU.mult))
            step(V.tensor_tensor(rec, rec, val, ALU.add))
            dve.sem_inc(s_rec, 1)
            step(V.tensor_tensor(onek, key[:, 0:C], key[:, 1:C + 1], ALU.is_gt))
            step(V.tensor_reduce(unsorted[:], onek, op=ALU.max, axis=AX.X))
            with dve.Fori(0, HIST_END) as u:
                steps.enter(u, 2 * KPT)

                def count_keys(j, r):
                    for k in ((r, KPT - 1) if r == R - 1 else (r,)):
                        at = ds(2 * KPT * u + KPT * j + k, 1)
                        step(V.tensor_scalar(onek, key[:, 0:C], iota_k[:, at], 0.0, op0=ALU.is_equal, op1=ALU.add,
                                             accum_out=hist[:, at]))

                pair(u, count_keys)
                steps.leave(HIST_END)
            dve.sem_inc(s_hist, 1)
            def over_k(t):
                return t.unsqueeze(1).broadcast_to([P, CG, NT])

            def over_g(t):
                return t.unsqueeze(2).broadcast_to([P, CG, NT])

            def chunk_tables(j, r):
                if j == 0:
                    return
                if r == 0:
                    dve.wait_ge(s_tot, 1)
                    step(V.tensor_copy(total[:], psM[0][:, 0:K]))
                    step(V.tensor_copy(base[:], psM[1][:, 0:K]))
                    step(V.tensor_copy(unsorted_i[:], psM[0][0:1, K:K + 1]))
                    step(V.tensor_scalar(total_i[:], total[:], float(P - 1), None, op0=ALU.add))
                elif r == 1:
                    step(V.tensor_scalar(total_i[:], total_i[:], 7, None, op0=ALU.arith_shift_right))
                    step(V.tensor_copy(nchunk[:], total_i[:]))
                    step(V.tensor_tensor_scan(cend[:], onesk[:], nchunk[:], 0.0, ALU.mult, ALU.add))
                    step(V.tensor_tensor_scan(eend[:], onesk[:], total[:], 0.0, ALU.mult, ALU.add))
                elif r == 2:
                    step(V.tensor_tensor(total[:], eend[:], total[:], ALU.subtract))
                    step(V.tensor_tensor(nchunk[:], cend[:], nchunk[:], ALU.subtract))
                    step(V.scalar_tensor_tensor(out=base[:], in0=base[:], scalar=-1.0, in1=total[:], op0=ALU.add, op1=ALU.add))
                    step(V.scalar_tensor_tensor(out=lag[:], in0=nchunk[:], scalar=-float(P), in1=total[:], op0=ALU.mult, op1=ALU.add))
                elif r == 3:
                    step(V.tensor_tensor(cmp[:, 0], over_g(chunk_of[:]), over_k(cend[:, 0:NT]), ALU.is_ge))
                    step(V.tensor_reduce(ctile[:], cmp[:, 0], op=ALU.add, axis=AX.X))
                elif r == 4:
                    step(V.tensor_tensor(cmp[:, 0], over_g(ctile[:]), over_k(iota_k[:, 0:NT]), ALU.is_equal))
                    step(V.tensor_tensor(cmp[:, 1], cmp[:, 0], over_k(lag[:, 0:NT]), ALU.mult))
                elif r == 5:
                    step(V.tensor_reduce(estart[:], cmp[:, 1], op=ALU.add, axis=AX.X))
                    step(V.scalar_tensor_tensor(out=estart[:], in0=chunk_of[:], scalar=float(P), in1=estart[:], op0=ALU.mult, op1=ALU.add))
                    step(V.tensor_scalar(estart[:], estart[:], float(C * P), None, op0=ALU.min))
                    step(V.tensor_copy(estart_i[:], estart[:]))
                elif r == 6:
                    step(V.tensor_tensor(cmp[:, 1], cmp[:, 0], over_k(eend[:, 0:NT]), ALU.mult))
                    step(V.tensor_reduce(nvalid[:], cmp[:, 1], op=ALU.add, axis=AX.X))
                    step(V.tensor_tensor(nvalid[:], nvalid[:], estart[:], ALU.subtract))
                elif r == 7:
                    step(V.tensor_scalar(ctile[:], ctile[:], float(NT - 1), None, op0=ALU.min))
                    for g in range(CG):
                        V.tensor_scalar(diag[:, g, :], ident[:], ctile[:, g:g + 1], None, op0=ALU.mult).then_inc(s_dve, 1)
                    steps.count += CG - 1
                    step(None)
                    dve.sem_inc(s_tab, 1)

            pair(HIST_END, chunk_tables)
            is_unsorted = dve.value_load(unsorted_i[0:1, 0:1], min_val=0, max_val=P)
            with dve.If(is_unsorted > 0):
                sort = Steps(dve, s_dveu)
                with dve.Fori(0, K) as k:
                    sort.enter(k, 4)
                    sort.step(V.tensor_scalar(onek, key[:, 0:C], iota_k[:, ds(k, 1)], None, op0=ALU.is_equal))
                    sort.step(V.tensor_tensor_scan(cum, onesc, onek, 0.0, ALU.mult, ALU.add))
                    sort.step(V.scalar_tensor_tensor(out=val, in0=cum, scalar=base[:, ds(k, 1)], in1=onek,
                                                     op0=ALU.add, op1=ALU.mult))
                    sort.step(V.tensor_tensor(pos, pos, val, ALU.add))
                    sort.leave(K)
                sort.step(V.tensor_copy(pos_i, pos))
                dve.sem_inc(s_pos, 1)
            with dve.Else():
                dve.nop()
            pair(HIST_END + 1)
            dve.wait_ge(s_tiles, 1)
            step(V.tensor_copy(run[:, 0:4 * P], psM[0][:]))
            step(V.tensor_copy(run[:, 4 * P:NCP], psM[1][:, 0:NCP - 4 * P]))
            tiles_p = tile_i.rearrange("o (m b) -> o b m", b=2)
            first, second = run[0:1, 0:STREAM], run[0:1, STREAM:2 * STREAM]
            shared = run[0:1, STREAM - 1:STREAM]
            step(V.tensor_copy(tiles_p[:, 0], first))
            step(V.tensor_copy(shared_i[:], shared))
            step(V.tensor_scalar(gap[:], shared, -1.0, float(NT), op0=ALU.mult, op1=ALU.add))
            step(V.tensor_scalar(relT[0:1, 0:STREAM], second, shared, None, op0=ALU.is_equal))
            step(V.scalar_tensor_tensor(out=tiles_p[:, 1], in0=relT[0:1, 0:STREAM], scalar=gap[:], in1=second, op0=ALU.mult, op1=ALU.add))
            step(V.memset(same_prev, 0.0))
            step(V.memset(same_next, 0.0))
            step(V.tensor_tensor(same_prev[:, 1:NCP], run[:, 1:NCP], run[:, 0:NCP - 1], ALU.is_equal))
            step(V.tensor_tensor(same_next[:, 0:NCP - 1], run[:, 0:NCP - 1], run[:, 1:NCP], ALU.is_equal))
            dve.wait_ge(s_slotg, 16 * CG)
            slot3 = slotc.rearrange("p (g e) -> p g e", g=CG)
            valid3 = relT.rearrange("p (g e) -> p g e", g=CG)
            step(V.tensor_tensor(valid3, iota_row[:].unsqueeze(1).broadcast_to([P, CG, P]),
                                 nvalid[:].unsqueeze(2).broadcast_to([P, CG, P]), ALU.is_lt))
            step(V.scalar_tensor_tensor(out=slotc, in0=slotc, scalar=-INVALID, in1=relT, op0=ALU.add, op1=ALU.mult))
            step(V.tensor_scalar(slotc, slotc, INVALID, None, op0=ALU.add))
            step(V.tensor_copy(slotc_i, slotc))
            step(V.tensor_scalar(slotc_i, slotc_i, 16, None, op0=ALU.arith_shift_right))
            step(V.tensor_copy(rowc, slotc_i))
            dve.sem_inc(s_rowc, 1)
            pair(HIST_END + 2)
            dve.wait_ge(s_slotT, 1)
            step(V.tensor_copy(rec_i[:, 0:4 * P], psM[0][:]))
            step(V.tensor_copy(rec_i[:, 4 * P:NCP], psM[1][:, 0:NCP - 4 * P]))
            step(V.memset(gidx[:, CPT * NT:], 0))
            step(V.tensor_scalar(gidx[:, 0:CPT * NT].rearrange("p (m b) -> p b m", b=2),
                                 rec_i[:, 0:2 * STREAM].rearrange("p (b m) -> p b m", b=2), 65535, None, op0=ALU.bitwise_and))
            step(V.tensor_scalar(slotc_i, rec_i, R - 1, None, op0=ALU.bitwise_and))
            step(V.tensor_copy(relT, slotc_i))
            step(V.tensor_scalar(slotc_i, rec_i, 16, None, op0=ALU.arith_shift_right))
            step(V.tensor_copy(rowT[:], slotc_i))
            step(V.memset(rowP[:, CPT * NT:], 0.0))
            step(V.tensor_copy(rowP[:, 0:CPT * NT].rearrange("p (m b) -> p b m", b=2),
                               slotc_i[:, 0:2 * STREAM].rearrange("p (b m) -> p b m", b=2)))
            dve.wait_ge(s_recst, 32)
            step(V.tensor_tensor(rel1, relT.unsqueeze(2).broadcast_to([P, NCP, R]),
                                 iota_k[:, 0:R].unsqueeze(1).broadcast_to([P, NCP, R]), ALU.is_equal))
            dve.wait_ge(s_rowst, 16)

            def rows_one_hot(dest, c0, n, rows=rowT):
                return V.tensor_tensor(dest, rows[:, ds(c0, n)].unsqueeze(2).broadcast_to([P, n, P]),
                                       iota_row[:].unsqueeze(1).broadcast_to([P, n, P]), ALU.is_equal)

            with dve.Fori(COUNT, SCAN) as u:
                def one_hots(j, r):
                    if r % 2 == 0:
                        g = 8 * (u - COUNT) + 4 * j + r // 2
                        dve.wait_ge(s_cnt, g + 1)
                        V.tensor_copy(relg[:, r // 2 % 2], rel1[:, ds(g * GC, GC), :]).then_inc(s_D1, 1)
                        rows_one_hot(D1[:, r // 2 % 2], g * GC, GC).then_inc(s_D1, 1)

                pair(u, before=one_hots)
            dve.wait_ge(s_cntc, 2 + NCP // GC)
            dve.wait_ge(s_cnt, 2 + NCP // GC)
            with dve.Fori(SCAN, LOOK) as u:
                steps.enter(u - SCAN, 2 * 8)

                def invert(j, r):
                    rel = 2 * (u - SCAN) + j
                    mine = cnt[:, ds(rel, 1), :].rearrange("p r c -> p (r c)")
                    high = inv[:, ds(rel, 1), 0, :].rearrange("p r c -> p (r c)")
                    low = inv[:, ds(rel, 1), 1, :].rearrange("p r c -> p (r c)")
                    if r == 0:
                        step(V.tensor_tensor_scan(run, same_prev, mine, 0.0, ALU.mult, ALU.add))
                    elif r == 1:
                        step(V.tensor_tensor(tmpc, run, same_next, ALU.mult))
                    elif r == 2:
                        step(V.tensor_tensor(tmpc, run, tmpc, ALU.subtract))
                    elif r == 3:
                        step(V.tensor_tensor_scan(run[:, ::-1], same_next[:, ::-1], tmpc[:, ::-1], 0.0, ALU.mult, ALU.add))
                    elif r == 4:
                        step(V.tensor_scalar(run, run, 1.0, None, op0=ALU.max))
                        step(V.reciprocal(tmpc, run))
                    elif r == 6:
                        step(V.tensor_scalar(high, tmpc, SWT, None, op0=ALU.mult))
                    elif r == 7:
                        step(V.scalar_tensor_tensor(out=low, in0=tmpc, scalar=SWT, in1=high, op0=ALU.mult, op1=ALU.subtract))

                pair(u, invert)
                steps.leave(LOOK - SCAN)
            dve.sem_inc(s_inv, 1)
            with dve.Fori(LOOK, PAIRS) as u:
                steps.enter(u - LOOK, 8)

                def weights(j, r):
                    g = 8 * (u - LOOK) + 4 * j + r // 2
                    q = r // 2 % 2
                    if r % 2 == 0:
                        dve.wait_ge(s_rb[q], 16 * (4 * (u - LOOK) + 2 * j + r // 4 + 1))
                        dve.wait_ge(s_look, g + 1)
                        V.tensor_scalar(D1[:, q], rows_b[:, q], iota_part[:, 0:1], None, op0=ALU.is_equal).then_inc(s_DT, 1)
                    else:
                        dve.wait_ge(s_look, 2 + g + 1)
                        step(V.tensor_tensor(prod, psM[q][:, 0:GC * 2 * R].rearrange("p (c r q) -> p c r q", q=2, r=R),
                                             rel1[:, ds(g * GC, GC), :].unsqueeze(3).broadcast_to([P, GC, R, 2]), ALU.mult))
                        V.tensor_reduce(wgt[:, ds(g * GC, GC), :], prod.rearrange("p c r q -> p c q r"),
                                        op=ALU.add, axis=AX.X).then_inc(s_w8, 1)

                pair(u, weights)
                steps.leave(PAIRS - LOOK)
            dve.wait_ge(s_bias, 16)
            dve.wait_ge(s_w8, 2 + NCP // GC)
            V.memset(acc[:, NT, :], 0.0).then_inc(s_accz, 1)
            with dve.Fori(0, (ACC_SPLIT - 2 * UNDER_H) // 2) as i:
                for j in range(2):
                    V.tensor_copy(flat(acc[:, ds(2 * UNDER_H + 2 * i + j, 1), :]), biasb[:]).then_inc(s_accz, 1)
            h_low(0, NT - 1)

            dve.wait_ge(s_h, R * NT)
            rows_one_hot(dgrp[:, 0], 0, HALF, rowP).then_inc(s_D, 1)
            dve.wait_ge(s_st[0], 16 * (PAIRS + 1))
            for t in range(UNDER_H // 2):
                V.tensor_copy(acc[:, t, :], biasb[:]).then_inc(s_accz, 1)
            dve.wait_ge(s_accz, NT + 1)
            with dve.Fori(0, NT) as i:
                _, tiles = nc.values_load_multi_w_load_instructions(
                    tile_i[0:1, ds(CPT * i, CPT)], engines=(mybir.EngineType.DVE,), min_val=0, max_val=NT,
                    skip_runtime_bounds_check_because="the chunk tables hold tiles up to NT - 1, and NT for the spare")
                for s in range(CPT):
                    c = CPT * i + s
                    if s % HALF == 0:
                        a = s // HALF
                        dve.wait_ge(s_S, HALF * (2 * i + a + 1))
                        rows_one_hot(dgrp[:, 1 - a], c + HALF, HALF, rowP).then_inc(s_D, 1)
                    dve.wait_ge(s_mm, BANKS + c + 1)
                    dve.wait_ge(s_acc, BANKS - 1 + c)
                    row = flat(acc[:, ds(tiles[s], 1), :])
                    V.scalar_tensor_tensor(out=row, in0=ps2[s % BANKS][:], scalar=1.0 / (SH * SWT), in1=row,
                                           op0=ALU.mult, op1=ALU.add).then_inc(s_acc, 1)
                    if s == 9:
                        dve.wait_ge(s_x2hi, i + 1)
                        V.scalar_tensor_tensor(out=xT[:, 0, 1, :], in0=psT[0][:], scalar=SX, in1=xT[:, 0, 0, :],
                                               op0=ALU.mult, op1=ALU.subtract).then_inc(s_x2lo, 1)
                    if s == 16:
                        dve.wait_ge(s_self, i + 1)
                        dve.wait_ge(s_acc, BANKS + c + 1)
                        own = flat(acc[:, ds(i, 1), :])
                        V.scalar_tensor_tensor(out=own, in0=psT[1][:], scalar=1.0 / (SX * SW), in1=own,
                                               op0=ALU.mult, op1=ALU.add).then_inc(s_selfa, 1)
                        dve.wait_ge(s_selfa, 1 + i + 1)
            dve.wait_ge(s_acc, BANKS + CPT * NT)
            shared_tile = dve.value_load(shared_i[0:1, 0:1], min_val=0, max_val=NT - 1)
            shared_acc = flat(acc[:, ds(shared_tile, 1), :])
            V.tensor_tensor(shared_acc, shared_acc, acc[:, NT, :], ALU.add).then_inc(s_merged, 1)
            dve.wait_ge(s_merged, 1)
            def moments(lo, hi):
                with dve.Fori(0, (hi - lo) // 4) as i:
                    for j in range(4):
                        t = lo + 4 * i + j
                        V.bn_stats(flat(stats[:, ds(t, 1), :]), flat(acc[:, ds(t, 1), :])).then_inc(s_dve, 1)
                for t in range(lo + (hi - lo) // 4 * 4, hi):
                    V.bn_stats(stats[:, t, :], acc[:, t, :]).then_inc(s_dve, 1)
                steps.count += hi - lo - 1
                step(None)
                m0, m1, q0, q1 = (stats[:, lo:hi, n] for n in (1, 4, 2, 5))
                mu, v, nb = mean[:, lo:hi], var[:, lo:hi], nbias[:, lo:hi]
                step(V.tensor_tensor(nb, m0, m1, ALU.subtract))
                step(V.tensor_tensor(v, q0, q1, ALU.add))
                step(V.scalar_tensor_tensor(out=nb, in0=nb, scalar=0.25, in1=nb, op0=ALU.mult, op1=ALU.mult))
                step(V.scalar_tensor_tensor(out=v, in0=v, scalar=1.0 / D, in1=nb, op0=ALU.mult, op1=ALU.add))
                step(V.tensor_scalar(v, v, EPS, None, op0=ALU.add))
                dve.sem_inc(s_mv, 1)
                step(V.tensor_tensor(mu, m0, m1, ALU.add))
                step(V.tensor_scalar(mu, mu, 0.5, None, op0=ALU.mult))

            def inverses(k, lo, hi):
                mu, rs, nb = mean[:, lo:hi], rstd[:, lo:hi], nbias[:, lo:hi]
                dve.wait_ge(s_std, k)
                step(V.reciprocal(rs, rs))
                step(V.scalar_tensor_tensor(out=nb, in0=mu, scalar=-1.0, in1=rs, op0=ALU.mult, op1=ALU.mult))
                dve.sem_inc(s_rstd, 1)

            def normalise(t):
                row = flat(acc[:, ds(t, 1), :])
                V.tensor_scalar(row, row, mean[:, ds(t, 1)], rstd[:, ds(t, 1)],
                                op0=ALU.subtract, op1=ALU.mult).then_inc(s_y[0], 1)

            moments(0, NORM)
            inverses(1, 0, NORM)
            moments(NORM, NT)
            inverses(2, NORM, NT)
            with dve.Fori(0, (NT - NORM) // 4) as i:
                for j in range(2):
                    normalise(NORM + 4 * i + 2 * j)
            V.tensor_scalar(acc[:, NT - 1, :], acc[:, NT - 1, :], mean[:, NT - 1:NT], rstd[:, NT - 1:NT],
                            op0=ALU.subtract, op1=ALU.mult).then_inc(s_y[0], 1)


class Steps:

    def __init__(self, engine, semaphore):
        self.engine, self.semaphore = engine, semaphore
        self.count, self.before = 0, 0

    def step(self, instruction):
        self.count += 1
        if instruction is not None:
            instruction.then_inc(self.semaphore, 1)
        self.engine.wait_ge(self.semaphore, self.before + self.count)

    def enter(self, i, per):
        self.outside, self.per = self.count, per
        self.before = i * per

    def leave(self, turns):
        assert self.count - self.outside == self.per, (self.count, self.outside, self.per)
        self.count = self.outside + turns * self.per
        self.before = 0


def kernel(**inputs):
    import numpy as np
    import concourse.bacc as bacc
    from concourse.bass_utils import run_bass_kernel_spmd

    nc = bacc.Bacc("TRN2", target_bir_lowering=False, num_devices=1)
    arrays, args = {}, []
    for name in ("x", "src", "dst", "edge_type_8", "L0_gnn_W_self", "L0_gnn_W_rel", "L0_gnn_bias"):
        a = np.ascontiguousarray(inputs[name])
        arrays["in_" + name] = a
        args.append(nc.dram_tensor("in_" + name, a.shape, mybir.dt.from_np(a.dtype), kind="ExternalInput").ap())
    out = nc.dram_tensor("out", arrays["in_x"].shape, mybir.dt.float32, kind="ExternalOutput").ap()
    build_gnn(nc, *args, out)
    return run_bass_kernel_spmd(nc, [arrays], core_ids=[0]).results[0]["out"]
```

```python
import concourse.bass as bass
from concourse import mybir
from contextlib import ExitStack


def build_gnn(nc, x, src, dst, etype, w_self, w_rel, bias, out):
    f32, f16, i32 = mybir.dt.float32, mybir.dt.float16, mybir.dt.int32
    ALU, ACT, AX = mybir.AluOpType, mybir.ActivationFunctionType, mybir.AxisListType
    ds = bass.ds

    P = 128
    N, D = x.shape
    R = w_rel.shape[0]
    E = src.shape[0]
    KB = D // P
    NT = -(-N // P)
    LAST = N - (NT - 1) * P
    PAIRS = (NT - 1) // 2
    C = -(-E // P)
    C = -(-C // NT) * NT
    SC = C // NT
    E_LAST = E - (P - 1) * C
    CPT = -(-((E + NT * (P - 1)) // P) // NT)
    HALF = CPT // 2
    STREAM = CPT * NT // 2
    CG = -(-(CPT * NT) // P)
    NCP = CG * P
    GC = 16
    INVALID = float(P << 16)
    EPS = 1e-5
    SX, SW, SH, SWT = 2.0 ** 6, 2.0 ** 10, 2.0 ** 6, 2.0 ** 15
    LASTST = 4
    UNDER_H = R * 2 * D * 2 // (4 * D)
    EARLY = 12
    LATE = 2 * UNDER_H + EARLY + (NT - 2 * UNDER_H - 2 * EARLY + 1) // 2
    NORM = NT // 2
    BANKS = 6

    HIST_END = 3
    KPT = 9
    K = HIST_END * 2 * KPT
    COUNT = 6
    SCAN = COUNT + NCP // GC // 8
    LOOK = SCAN + R // 2
    assert E_LAST > 0 and 2 * PAIRS + 1 == NT and NORM % 4 == 0 and (NT - NORM) % 4 == 1 and CPT % BANKS == 0 and CPT % 2 == 0
    assert K > NT and LOOK + NCP // GC // 8 <= PAIRS and NCP % (8 * GC) == 0

    h = nc.dram_tensor("h_parts", [N * R, 2 * D], f16, kind="Internal").ap()
    h_rows = h.rearrange("(n r) d -> n (r d)", r=R)
    records = nc.dram_tensor("records", [C * P + P, 1], f32, kind="Internal").ap()
    rowids = nc.dram_tensor("sorted_rows", [NCP * P], f16, kind="Internal").ap()

    ctx = ExitStack()
    with ctx:
        def sb(name, shape, dt):
            return ctx.enter_context(nc.sbuf_tensor(name, shape, dt))

        def sem(name):
            return ctx.enter_context(nc.semaphore(name))

        w_all = sb("w_all", [P, R + 1, KB, 2, D], f16)
        wrel, wself = w_all[:, 0:R], w_all[:, R]
        xst = sb("xst", [P, 2, D], f32)
        xT = sb("xT", [P, 2, 2, KB * P], f16)
        arena = sb("arena", [P, (NT + 1) * D], f32)
        gidx = sb("gidx", [P, CPT * NT + HALF], i32)
        rowT = sb("rowT", [P, NCP], f16)
        wgt = sb("wgt", [P, NCP, 2], f32)
        onehot = sb("onehot", [P, BANKS, 2, P], f16)
        rowP = sb("rowP", [P, CPT * NT + HALF], f16)
        tile_i = sb("tile_i", [1, CPT * NT], i32)
        shared_i = sb("shared_i", [1, 1], i32)
        gap = sb("gap", [1, 1], f32)
        ident = sb("ident", [P, P], f32)
        before = sb("before", [P, P], f32)
        ones = sb("ones", [P, P], f32)
        iota_row = sb("iota_row", [P, P], f16)
        iota_part = sb("iota_part", [P, 1], f32)
        iota_k = sb("iota_k", [P, K], f32)
        chunk_of = sb("chunk_of", [P, CG], f32)
        idx_a = sb("idx_a", [P, max(SC, CPT)], i32)
        rec_a = sb("rec_a", [P, SC], f32)
        padrec = sb("padrec", [1, P], f32)
        biasb = sb("biasb", [P, D], f32)
        hist = sb("hist", [P, K], f32)
        total = sb("total", [P, K], f32)
        total_i = sb("total_i", [P, K], i32)
        nchunk = sb("nchunk", [P, K], f32)
        cend = sb("cend", [P, K], f32)
        eend = sb("eend", [P, K], f32)
        lag = sb("lag", [P, K], f32)
        base = sb("base", [P, K], f32)
        onesk = sb("onesk", [P, K], f32)
        unsorted = sb("unsorted", [P, 1], f32)
        unsorted_i = sb("unsorted_i", [1, 1], i32)
        ctile = sb("ctile", [P, CG], f32)
        estart = sb("estart", [P, CG], f32)
        estart_i = sb("estart_i", [P, CG], i32)
        nvalid = sb("nvalid", [P, CG], f32)

        acc = arena[:, :].rearrange("p (t d) -> p t d", d=D)
        used = [0]

        def view(n, dt, at=None):
            size = {f32: 4, i32: 4, f16: 2}[dt] * n
            start = used[0] if at is None else at
            used[0] = start + size
            assert start % 4 == 0 and size % 4 == 0 and used[0] <= (NT + 1) * D * 4, (start, size)
            v = arena[:, start // 4:(start + size) // 4]
            return v if dt == f32 else v.bitcast(dt)

        hst = view(2 * R * 2 * D, f16).rearrange("p (j r c d) -> p j r c d", j=2, r=R, c=2)
        counts_at = used[0]
        cnt = view(R * NCP, f32).rearrange("p (r c) -> p r c", r=R)
        inv = view(R * 2 * NCP, f16, at=counts_at).rearrange("p (r q c) -> p r q c", r=R, q=2)
        relK = view(NCP, f16)
        dbuf_at = counts_at + 4 * R * NCP + 2 * R * NCP
        D1 = view(2 * GC * P, f16, at=dbuf_at).rearrange("p (j c d) -> p j c d", j=2, c=GC)
        rows_b = view(2 * GC * P, f16).rearrange("p (j c d) -> p j c d", j=2, c=GC)
        same_prev = view(NCP, f16)
        same_next = view(NCP, f16)
        run = view(NCP, f32)
        relg = view(2 * GC * R, f16).rearrange("p (j c r) -> p j c r", j=2, r=R)
        invg = view(2 * GC * 2 * R, f16).rearrange("p (j c q) -> p j c q", j=2, q=2 * R)
        prod = view(GC * 2 * R, f32).rearrange("p (c r q) -> p c r q", q=2, r=R)
        even = -(-(C + 1) // 2) * 2
        key = view(even, f16, at=counts_at)[:, 0:C + 1]
        onek = view(even, f16)[:, 0:C]
        cum = view(even, f16)[:, 0:C]
        onesc = view(even, f16)[:, 0:C]
        pos = view(C, f32)
        rec = view(C, f32)
        val = view(C, f32)
        dst_i = view(C + 1, i32)
        src_i = view(C, i32)
        et_i = view(C, i32)
        tmp_i = view(C + 1, i32)
        pos_i = view(C, i32)
        assert used[0] <= dbuf_at
        wst = view(2 * KB * D, f32, at=dbuf_at).rearrange("p (j b i) -> p j b i", j=2, b=KB)
        slotc = view(NCP, f32, at=dbuf_at)
        slotc_i = view(NCP, i32)
        rowc = view(NCP, f16)
        rec_at = used[0]
        rec_i = view(NCP, i32)
        relT = view(NCP, f32)
        diag = view(NCP, f32, at=rec_at).rearrange("p (g e) -> p g e", g=CG)
        tmpc = view(NCP, f32, at=dbuf_at)
        cmp = view(2 * CG * NT, f32, at=dbuf_at).rearrange("p (a g k) -> p a g k", a=2, g=CG)
        gath = wrel[:, 0:5].rearrange("p r k a d -> p (r k a d)")[:, 0:CPT * 2 * D].rearrange(
            "p (b q d) -> p b q d", b=CPT, q=2)
        dgrp = wrel[:, 5].rearrange("p k a d -> p (k a d)")[:, 0:2 * HALF * P].rearrange(
            "p (j c d) -> p j c d", j=2, c=HALF)
        stat = wrel[:, 7].rearrange("p k a d -> p (k a d)").bitcast(f32)
        stats = stat[:, 0:6 * NT].rearrange("p (t s) -> p t s", s=6)
        mean, var, rstd, nbias = (stat[:, (6 + n) * NT:(7 + n) * NT] for n in range(4))

        psT = [ctx.enter_context(nc.psum_tensor(f"psT{j}", [P, D], f32)) for j in range(2)]
        psH = [ctx.enter_context(nc.psum_tensor(f"psH{j}", [P, D], f32)) for j in range(4)]
        psM = [ctx.enter_context(nc.psum_tensor(f"psM{j}", [P, D], f32)) for j in range(2)]
        ps2 = psH + psM

        s_const = sem("consts_made")
        s_clear = sem("matrices_cleared")
        s_iota = sem("iotas_made")
        s_edges = sem("edges_loaded")
        s_blank = sem("edge_buffers_padded")
        s_bias = sem("bias_loaded")
        s_w = [sem(f"w_loaded{j}") for j in range(2)]
        s_wT = sem("w_transposed")
        s_whi = sem("w_high_made")
        s_wlo = sem("w_low_made")
        s_dve = sem("dve_step")
        s_dveu = sem("dve_sort_step")
        s_x = [sem(f"x_loaded{j}") for j in range(2)]
        s_xT = sem("x_transposed")
        s_xhi = sem("x_high_made")
        s_xlo = sem("x_low_made")
        s_h = sem("h_summed")
        s_hhi = sem("h_high_made")
        s_hlo = sem("h_low_made")
        s_st = [sem(f"h_stored{j}") for j in range(2)]
        s_rec = sem("records_made")
        s_recst = sem("records_stored")
        s_hist = sem("histogram_made")
        s_tot = sem("totals_summed")
        s_tab = sem("chunk_tables_made")
        s_tiles = sem("chunk_tiles_broadcast")
        s_pos = sem("positions_ready")
        s_stage = sem("scatter_staged")
        s_sc = [sem(f"scattered{j}") for j in range(SC)]
        s_slotg = sem("slots_gathered")
        s_rowc = sem("slots_masked")
        s_slotT = sem("slots_transposed")
        s_rowst = sem("rowids_stored")
        s_folded = sem("identity_added")
        s_D1 = sem("count_operands_made")
        s_cnt = sem("group_counted")
        s_cntc = sem("counts_copied")
        s_inv = sem("inverses_made")
        s_rb = [sem(f"rows_broadcast{j}") for j in range(2)]
        s_invg = sem("group_inverses_copied")
        s_DT = sem("transposed_one_hots_made")
        s_look = sem("group_looked_up")
        s_w8 = sem("weights_made")
        s_go = sem("pool_waits_passed")
        s_accz = sem("acc_initialised")
        s_idx = sem("indices_staged")
        s_g = [sem(f"gathered{b}") for b in range(CPT)]
        s_D = sem("edge_one_hots_made")
        s_S = sem("edge_weights_placed")
        s_mm = sem("chunk_summed")
        s_acc = sem("chunk_added")
        s_x2 = sem("x_reloaded")
        s_x2T = sem("x2_transposed")
        s_x2hi = sem("x2_high_made")
        s_x2lo = sem("x2_low_made")
        s_self = sem("self_summed")
        s_merged = sem("spare_added")
        s_selfa = sem("self_added")
        s_mv = sem("moments_made")
        s_std = sem("deviation_made")
        s_rstd = sem("scales_made")
        s_y1 = sem("first_tiles_normalised")
        s_y = [sem(f"normalised_by_{e}") for e in ("dve", "act")]
        s_out = sem("out_stored")

        block = ctx.enter_context(nc.Block())

        def flat(t):
            return t.rearrange("p a b -> p (a b)")

        @block.sync
        def _(sp):
            sp.dma_start(xst[:, 0], x[0:P, :]).then_inc(s_x[0], 16)
            sp.dma_start(wst[:, 0], w_rel[0].rearrange("(b p) i -> p b i", p=P)).then_inc(s_w[0], 16)
            sp.dma_start(wst[:, 1], w_rel[1].rearrange("(b p) i -> p b i", p=P)).then_inc(s_w[1], 16)
            sp.dma_start(xst[:, 1], x[P:2 * P, :]).then_inc(s_x[1], 16)
            with sp.Fori(1, R // 2) as u:
                for j in range(2):
                    sp.wait_ge(s_wT, KB * (2 * u + j - 1))
                    sp.dma_start(wst[:, j], w_rel[ds(2 * u + j, 1)].rearrange("r (b p) i -> p (r b) i", p=P)).then_inc(s_w[j], 16)
            sp.wait_ge(s_wT, KB * (R - 1))
            sp.dma_start(wst[:, 0], w_self.rearrange("(b p) i -> p b i", p=P)).then_inc(s_w[0], 16)
            sp.wait_ge(s_blank, 1)
            dst_rows = bass.AP(tensor=dst.tensor, offset=dst.offset, ap=[[C, P - 1], [1, C + 1]])
            sp.dma_start(dst_i[0:P - 1, :], dst_rows).then_inc(s_edges, 16)
            sp.dma_start(dst_i[P - 1:P, 0:E_LAST], dst[(P - 1) * C:E].rearrange("(p c) -> p c", p=1)).then_inc(s_edges, 16)
            for arr, buf in ((src, src_i), (etype, et_i)):
                sp.dma_start(buf[0:P - 1, :], arr[0:(P - 1) * C].rearrange("(p c) -> p c", c=C)).then_inc(s_edges, 16)
                sp.dma_start(buf[P - 1:P, 0:E_LAST], arr[(P - 1) * C:E].rearrange("(p c) -> p c", p=1)).then_inc(s_edges, 16)
            sp.dma_start(biasb[:], bias.rearrange("(o d) -> o d", o=1).broadcast_to([P, D])).then_inc(s_bias, 16)

            def store_h(t, j, n=P):
                sp.wait_ge(s_hlo, 4 + R * (t + 1))
                sp.dma_start(h_rows[ds(t * P, n), :],
                             hst[0:n, j].rearrange("p r c d -> p (r c d)")).then_inc(s_st[j], 16)

            with sp.Fori(0, PAIRS - 1) as u:
                for j in range(2):
                    t = 2 * u + j
                    sp.wait_ge(s_xT, t + 1)
                    sp.dma_start(xst[:, j], x[ds((t + 2) * P, P), :]).then_inc(s_x[j], 16)
                    store_h(t, j)
            sp.wait_ge(s_xT, NT - 2)
            sp.dma_start(xst[0:LAST, 0], x[(NT - 1) * P:N, :]).then_inc(s_x[0], 16)
            store_h(NT - 3, 0)
            store_h(NT - 2, 1)
            for k in range(LASTST):
                rr = R // LASTST
                sp.wait_ge(s_hlo, 4 + R * (NT - 1) + rr * (k + 1))
                sp.dma_start(h_rows[(NT - 1) * P:N, k * rr * 2 * D:(k + 1) * rr * 2 * D],
                             hst[0:LAST, 0, k * rr:(k + 1) * rr].rearrange("p r c d -> p (r c d)")).then_inc(s_st[0], 16)
            with sp.Fori(0, NT - 1) as i:
                sp.wait_ge(s_x2lo, i + 1)
                sp.dma_start(xst[:, 0], x[ds(i * P, P), :]).then_inc(s_x2, 16)
            sp.wait_ge(s_x2lo, NT)
            sp.dma_start(xst[0:LAST, 0], x[(NT - 1) * P:N, :]).then_inc(s_x2, 16)
            def store_tiles(t):
                sp.dma_start(out[ds(t * P, 4 * P), :].rearrange("(t p) d -> p t d", p=P),
                             acc[:, ds(t, 4), :]).then_inc(s_out, 16)

            with sp.Fori(0, NORM // 4) as i:
                sp.wait_ge(s_y1, 4 * i + 4)
                store_tiles(4 * i)
            with sp.Fori(0, (NT - NORM) // 4) as i:
                sp.wait_ge(s_y[0], 2 * i + 2)
                sp.wait_ge(s_y[1], 2 * i + 2)
                store_tiles(NORM + 4 * i)
            sp.wait_ge(s_y[0], (NT - NORM) // 2 + 1)
            sp.dma_start(out[(NT - 1) * P:N, :], acc[0:LAST, NT - 1, :]).then_inc(s_out, 16)
            sp.wait_ge(s_out, 16 * (NT // 4 + 1))

        @block.tensor
        def _(pe):
            pe.wait_ge(s_const, 6)

            def w_transposes(j, n_w, g):
                pe.wait_ge(s_w[j], 16 * n_w)
                for k in range(KB):
                    pe.wait_ge(s_wlo, g + k + 1)
                    for b in range(KB):
                        last = nc.tensor.transpose(psH[k][:, b * P:(b + 1) * P], wst[:, j, b, k * P:(k + 1) * P], ident[:])
                    last.then_inc(s_wT, 1)

            def x_transposes(j, n_x, t):
                pe.wait_ge(s_x[j], 16 * n_x)
                pe.wait_ge(s_xlo, t + 1)
                for k in range(KB):
                    last = nc.tensor.transpose(psT[j][:, k * P:(k + 1) * P], xst[:, j, k * P:(k + 1) * P], ident[:])
                last.then_inc(s_xT, 1)

            def products(bank, j, w):
                for k in range(KB):
                    hi, lo = xT[:, j, 0, k * P:(k + 1) * P], xT[:, j, 1, k * P:(k + 1) * P]
                    nc.tensor.matmul(bank[:], hi, w[:, k, 0, :], start=(k == 0), stop=False)
                    nc.tensor.matmul(bank[:], hi, w[:, k, 1, :], start=False, stop=False)
                    last = nc.tensor.matmul(bank[:], lo, w[:, k, 0, :], start=False, stop=(k == KB - 1))
                return last

            def tile_products(j, t, group=None, g0=0):
                pe.wait_ge(s_xlo, 2 + t + 1)
                for r in range(R):
                    pe.wait_ge(s_hlo, R * t + r + 1)
                    products(psH[r % 4], j, wrel[:, r]).then_inc(s_h, 1)
                    if group and r % 2:
                        group(g0 + r // 2, r // 2 % 2)

            def next_and_product(r, j, n_w):
                w_transposes(1 - j, n_w, KB * (r + 1))
                pe.wait_ge(s_wlo, KB + KB * (r + 1))
                pe.wait_ge(s_hlo, 4 - 1 + r)
                products(psM[j], 0, wrel[:, ds(r, 1)].rearrange("p r k a d -> p (r k) a d")).then_inc(s_h, 1)

            x_transposes(0, 1, 0)
            w_transposes(0, 1, 0)
            pe.wait_ge(s_xlo, 2 + 1)
            with pe.Fori(0, R // 2 - 1) as u:
                next_and_product(2 * u, 0, u + 1)
                next_and_product(2 * u + 1, 1, u + 2)
            next_and_product(R - 2, 0, R // 2)
            pe.wait_ge(s_folded, KB)
            next_and_product(R - 1, 1, R // 2 + 1)
            pe.wait_ge(s_wlo, KB + KB * (R + 1))

            def pair(u, mid=None, group=None, g0=0):
                x_transposes(1, u + 1, 2 * u + 1)
                tile_products(0, 2 * u, group, g0)
                x_transposes(0, u + 2, 2 * u + 2)
                if mid:
                    mid()
                tile_products(1, 2 * u + 1, group, g0 + 4)

            def totals():
                pe.wait_ge(s_hist, 1)
                nc.tensor.matmul(psM[0][:, 0:K], ones[:], hist[:], start=True, stop=True)
                nc.tensor.matmul(psM[0][:, K:K + 1], ones[:], unsorted[:], start=True, stop=True)
                nc.tensor.matmul(psM[1][:, 0:K], before[:], hist[:], start=True, stop=True).then_inc(s_tot, 1)

            def chunk_tiles():
                pe.wait_ge(s_tab, 1)
                for g in range(CG):
                    last = nc.tensor.matmul(psM[g // 4][:, (g % 4) * P:(g % 4 + 1) * P], ones[:], diag[:, g, :],
                                            start=True, stop=True)
                last.then_inc(s_tiles, 1)

            def slot_transposes():
                pe.wait_ge(s_rowc, 1)
                for g in range(CG):
                    last = nc.tensor.transpose(psM[g // 4][:, (g % 4) * P:(g % 4 + 1) * P], slotc[:, g * P:(g + 1) * P], ident[:])
                last.then_inc(s_slotT, 1)

            def count(g, j):
                pe.wait_ge(s_D1, 2 * g + 2)
                pe.wait_ge(s_cntc, g + 1)
                for c in range(GC):
                    last = nc.tensor.matmul(psM[j][:, c * R:(c + 1) * R], D1[:, j, c, :],
                                            relg[:, j, c, :], start=True, stop=True)
                last.then_inc(s_cnt, 1)

            def look_up(g, j):
                pe.wait_ge(s_DT, 2 + g + 1)
                pe.wait_ge(s_invg, g + 1)
                pe.wait_ge(s_w8, g + 1)
                for c in range(GC):
                    last = nc.tensor.matmul(psM[j][:, c * 2 * R:(c + 1) * 2 * R], D1[:, j, c, :],
                                            invg[:, j, c, :], start=True, stop=True)
                last.then_inc(s_look, 1)

            x_transposes(1, 1, 1)
            x_transposes(0, 2, 2)
            tile_products(1, 1)
            with pe.Fori(1, HIST_END) as u:
                pair(u)
            pair(HIST_END, mid=totals)
            pair(HIST_END + 1, mid=chunk_tiles)
            pair(HIST_END + 2, mid=slot_transposes)
            with pe.Fori(COUNT, SCAN) as u:
                pair(u, group=count, g0=8 * (u - COUNT))
            with pe.Fori(SCAN, LOOK) as u:
                pair(u)
            with pe.Fori(LOOK, PAIRS) as u:
                pair(u, group=look_up, g0=8 * (u - LOOK))
            tile_products(0, NT - 1)

            pe.sem_inc(s_mm, BANKS)
            with pe.Fori(0, NT) as i:
                for s in range(CPT):
                    c = CPT * i + s
                    if s == 5:
                        pe.wait_ge(s_x2, 16 * (i + 1))
                        pe.wait_ge(s_x2lo, i + 1)
                        for k in range(KB):
                            last = nc.tensor.transpose(psT[0][:, k * P:(k + 1) * P], xst[:, 0, k * P:(k + 1) * P], ident[:])
                        last.then_inc(s_x2T, 1)
                    b = s % BANKS
                    pe.wait_ge(s_S, HALF + c + 1)
                    pe.wait_ge(s_acc, c + 1)
                    pe.wait_ge(s_g[s], 16 * (i + 1))
                    bank = ps2[b]
                    nc.tensor.matmul(bank[:], onehot[:, b, 0, :], gath[:, s, 0, :], start=True, stop=False)
                    nc.tensor.matmul(bank[:], onehot[:, b, 0, :], gath[:, s, 1, :], start=False, stop=False)
                    nc.tensor.matmul(bank[:], onehot[:, b, 1, :], gath[:, s, 0, :], start=False, stop=True).then_inc(s_mm, 1)
                    if s == 12:
                        pe.wait_ge(s_x2lo, i + 2)
                        pe.wait_ge(s_selfa, i + 1)
                        products(psT[1], 0, wself).then_inc(s_self, 1)

        @block.scalar
        def _(act):
            act.sem_inc(s_cntc, 2)

            def w_high(dest, g, k):
                act.wait_ge(s_wT, g + k + 1)
                nc.scalar.activation(dest, psH[k][:], ACT.Copy, scale=SW).then_inc(s_whi, 1)

            def x_high(j, t, reused=True):
                act.wait_ge(s_xT, t + 1)
                if reused:
                    act.wait_ge(s_h, R * (t - 1))
                nc.scalar.activation(xT[:, j, 0, :], psT[j][:], ACT.Copy, scale=SX).then_inc(s_xhi, 1)

            def h_high(j, t, reused=True, group=None, g0=0):
                for r in range(R):
                    act.wait_ge(s_h, R * t + r + 1)
                    if r == 0 and reused:
                        act.wait_ge(s_st[j], 8 * (t - j))
                    nc.scalar.activation(hst[:, j, r, 0, :], psH[r % 4][:], ACT.Copy,
                                         scale=SH / (SX * SW)).then_inc(s_hhi, 1)
                    if group and r % 2:
                        group(g0 + r // 2, r // 2 % 2)

            def copy_counts(g, j):
                act.wait_ge(s_cnt, 2 + g + 1)
                nc.scalar.activation(cnt[:, :, ds(g * GC, GC)],
                                     psM[j][:, 0:GC * R].rearrange("p (c r) -> p r c", r=R), ACT.Copy).then_inc(s_cntc, 1)

            def pair(u, **kw):
                g0 = kw.pop("g0", 0)
                x_high(0, 2 * u + 2)
                h_high(1, 2 * u + 1, g0=g0, **kw)
                x_high(1, 2 * u + 3)
                h_high(0, 2 * u + 2, g0=g0 + 4, **kw)

            x_high(0, 0, reused=False)
            for k in range(KB):
                w_high(w_all[:, 0, k, 0, :], 0, k)
            with act.Fori(0, R // 2) as u:
                for j in range(2):
                    r = 2 * u + j
                    for k in range(KB):
                        w_high(w_all[:, ds(r + 1, 1), k, 0, :].rearrange("p r d -> p (r d)"), (r + 1) * KB, k)
                    act.wait_ge(s_h, r + 1)
                    nc.scalar.activation(hst[:, 0, ds(r, 1), 0, :].rearrange("p r d -> p (r d)"), psM[j][:], ACT.Copy,
                                         scale=SH / (SX * SW)).then_inc(s_hhi, 1)
            x_high(1, 1, reused=False)
            x_high(0, 2)
            h_high(1, 1, reused=False)
            x_high(1, 3)
            h_high(0, 2)
            with act.Fori(1, COUNT - 1) as u:
                pair(u)
            x_high(0, 2 * COUNT)
            h_high(1, 2 * COUNT - 1)
            x_high(1, 2 * COUNT + 1)
            h_high(0, 2 * COUNT, group=copy_counts, g0=0)
            with act.Fori(COUNT, SCAN - 1) as u:
                pair(u, group=copy_counts, g0=8 * (u - COUNT) + 4)
            x_high(0, 2 * SCAN)
            h_high(1, 2 * SCAN - 1, group=copy_counts, g0=8 * (SCAN - COUNT) - 4)
            x_high(1, 2 * SCAN + 1)
            h_high(0, 2 * SCAN)
            with act.Fori(SCAN, PAIRS - 1) as u:
                pair(u)
            x_high(0, NT - 1)
            h_high(1, NT - 2)
            def start_as_bias(t):
                nc.scalar.activation(flat(acc[:, ds(t, 1), :]), biasb[:], ACT.Copy).then_inc(s_accz, 1)

            act.wait_ge(s_bias, 16)
            act.wait_ge(s_w8, 2 + NCP // GC)
            with act.Fori(0, EARLY // 4) as i:
                for k in range(4):
                    start_as_bias(NT - EARLY + 4 * i + k)
            h_high(0, NT - 1)
            nc.scalar.activation(idx_a[:, 0:HALF], gidx[:, 0:HALF], ACT.Copy).then_inc(s_idx, 1)
            for t in range(LATE, NT - EARLY):
                start_as_bias(t)
            act.wait_ge(s_st[1], 16 * PAIRS)
            for t in range(UNDER_H * 13 // 8, 2 * UNDER_H):
                start_as_bias(t)
            act.wait_ge(s_st[0], 16 * (PAIRS + LASTST))
            for t in range(UNDER_H * 5 // 8, UNDER_H):
                start_as_bias(t)

            with act.Fori(0, NT) as i:
                for s in range(CPT):
                    c = CPT * i + s
                    if s % HALF == 0:
                        act.wait_ge(s_D, 2 * i + s // HALF + 1)
                    sorted_c = HALF * i + s // 2 + s % 2 * STREAM
                    act.wait_ge(s_mm, c + 1)
                    for q in range(2):
                        ins = nc.scalar.activation(onehot[:, s % BANKS, q, :], dgrp[:, s // HALF, s % HALF, :],
                                                   ACT.Copy, scale=wgt[:, ds(sorted_c, 1), q])
                    ins.then_inc(s_S, 1)
                    if s == BANKS - 1:
                        nc.scalar.activation(idx_a[:, HALF:CPT], gidx[:, ds(c - s + HALF, HALF)], ACT.Copy).then_inc(s_idx, 1)
                    if s == HALF + BANKS - 1:
                        nc.scalar.activation(idx_a[:, 0:HALF], gidx[:, ds(c - s + CPT, HALF)], ACT.Copy).then_inc(s_idx, 1)
                    if s == 7:
                        act.wait_ge(s_x2T, i + 1)
                        act.wait_ge(s_selfa, i + 1)
                        nc.scalar.activation(xT[:, 0, 0, :], psT[0][:], ACT.Copy, scale=SX).then_inc(s_x2hi, 1)

            def normalise(t):
                row = flat(acc[:, ds(t, 1), :])
                return nc.scalar.activation(row, row, ACT.Identity, bias=nbias[:, ds(t, 1)], scale=rstd[:, ds(t, 1)])

            def deviation(k, lo, hi):
                act.wait_ge(s_mv, k)
                nc.scalar.activation(rstd[:, lo:hi], var[:, lo:hi], ACT.Sqrt).then_inc(s_std, 1)
                act.wait_ge(s_rstd, k)

            deviation(1, 0, NORM)
            with act.Fori(0, NORM // 4) as i:
                for j in range(4):
                    normalise(4 * i + j).then_inc(s_y1, 1)
            deviation(2, NORM, NT)
            with act.Fori(0, (NT - NORM) // 4) as i:
                for j in range(2):
                    normalise(NORM + 4 * i + 2 * j + 1).then_inc(s_y[1], 1)

        @block.gpsimd
        def _(pool):
            nc.gpsimd.memset(ident[:], 0.0).then_inc(s_clear, 1)
            nc.gpsimd.memset(before[:], 0.0).then_inc(s_clear, 1)
            pool.wait_ge(s_clear, 2)
            nc.gpsimd.affine_select(out=ident[:], in_=ident[:], compare_op=ALU.not_equal, fill=1.0, base=0,
                                    pattern=[[-1, P]], channel_multiplier=1).then_inc(s_const, 1)
            nc.gpsimd.affine_select(out=before[:], in_=before[:], compare_op=ALU.is_ge, fill=1.0, base=0,
                                    pattern=[[-1, P]], channel_multiplier=1).then_inc(s_const, 1)
            nc.gpsimd.memset(ones[:], 1.0).then_inc(s_const, 1)
            nc.gpsimd.memset(dst_i, NT * P).then_inc(s_const, 1)
            nc.gpsimd.memset(src_i, 0).then_inc(s_const, 1)
            nc.gpsimd.memset(et_i, 0).then_inc(s_const, 1)
            pool.wait_ge(s_const, 6)
            pool.sem_inc(s_blank, 1)
            nc.gpsimd.iota(iota_row[:], pattern=[[1, P]], base=0, channel_multiplier=0,
                           allow_small_or_imprecise_dtypes=True).then_inc(s_iota, 1)
            nc.gpsimd.iota(iota_part[:], pattern=[[0, 1]], base=0, channel_multiplier=1,
                           allow_small_or_imprecise_dtypes=True).then_inc(s_iota, 1)
            nc.gpsimd.iota(iota_k[:], pattern=[[1, K]], base=0, channel_multiplier=0,
                           allow_small_or_imprecise_dtypes=True).then_inc(s_iota, 1)
            nc.gpsimd.iota(chunk_of[:], pattern=[[P, CG]], base=0, channel_multiplier=1,
                           allow_small_or_imprecise_dtypes=True).then_inc(s_iota, 1)
            nc.gpsimd.memset(padrec[:], INVALID).then_inc(s_iota, 1)
            pool.wait_ge(s_rec, 1)
            pool.wait_ge(s_iota, 5)
            pool.dma_start(records[0:C * P, :].rearrange("(p c) o -> p (c o)", p=P), rec).then_inc(s_recst, 16)
            pool.dma_start(records[C * P:C * P + P, :].rearrange("(o e) i -> o (e i)", o=1), padrec[:]).then_inc(s_recst, 16)
            pool.wait_ge(s_recst, 32)
            pool.wait_ge(s_tab, 1)
            is_unsorted = pool.value_load(unsorted_i[0:1, 0:1], min_val=0, max_val=P)
            with pool.If(is_unsorted > 0):
                pool.wait_ge(s_pos, 1)

                def scatter(i, first=False):
                    for c in range(0 if first else SC):
                        pool.wait_ge(s_sc[c], i * 16)
                    nc.gpsimd.tensor_copy(idx_a[:, 0:SC], pos_i[:, ds(i * SC, SC)]).then_inc(s_stage, 1)
                    nc.gpsimd.tensor_copy(rec_a[:], rec[:, ds(i * SC, SC)]).then_inc(s_stage, 1)
                    pool.wait_ge(s_stage, 2 * i + 2)
                    pool.sem_inc(s_go, 1)
                    for c in range(SC):
                        nc.gpsimd.indirect_dma_start(
                            out=records[:, :], out_offset=bass.IndirectOffsetOnAxis(ap=idx_a[:, c:c + 1], axis=0),
                            in_=rec_a[:, c:c + 1], in_offset=None).then_inc(s_sc[c], 16)

                scatter(0, first=True)
                with pool.Fori(1, NT) as i:
                    scatter(i)
                for c in range(SC):
                    pool.wait_ge(s_sc[c], 16 * NT)
                pool.sem_inc(s_go, 1)
            with pool.Else():
                pool.sem_inc(s_go, 1)
            for g in range(CG):
                nc.gpsimd.indirect_dma_start(
                    out=slotc[:, g * P:(g + 1) * P], out_offset=None, in_=records[:, :],
                    in_offset=bass.IndirectOffsetOnAxis(ap=estart_i[:, g:g + 1], axis=0)).then_inc(s_slotg, 16)
            pool.wait_ge(s_rowc, 1)
            pool.dma_start(rowids.rearrange("(g p e) -> p g e", p=P, e=P),
                           rowc.rearrange("p (g e) -> p g e", g=CG)).then_inc(s_rowst, 16)
            pool.wait_ge(s_rowst, 16)
            pool.wait_ge(s_D1, 1)
            with pool.Fori(0, NCP // GC // 2) as i:
                for j in range(2):
                    pool.wait_ge(s_DT, 2 * i + j + 1)
                    pool.sem_inc(s_go, 1)
                    pool.dma_start(rows_b[:, j].rearrange("p c d -> p (c d)"),
                                   rowids[ds((2 * i + j) * (GC * P), GC * P)].rearrange("(o e) -> o e", o=1)
                                   .broadcast_to([P, GC * P])).then_inc(s_rb[j], 16)
                    pool.wait_ge(s_inv, 1)
                    pool.wait_ge(s_look, 2 * i + j + 1)
                    nc.gpsimd.tensor_copy(invg[:, j].rearrange("p c q -> p q c"),
                                          inv[:, :, :, ds((2 * i + j) * GC, GC)].rearrange("p r q c -> p (r q) c")
                                          ).then_inc(s_invg, 1)
            pool.wait_ge(s_st[0], 16 * (PAIRS + LASTST))
            pool.wait_ge(s_st[1], 16 * PAIRS)
            pool.wait_ge(s_w8, 2 + NCP // GC)

            def gathers(i):
                for a in range(2):
                    pool.wait_ge(s_idx, 2 * i + a + 1)
                    pool.sem_inc(s_go, 1)
                    for s in range(a * HALF, (a + 1) * HALF):
                        nc.gpsimd.indirect_dma_start(
                            out=gath[:, s].rearrange("p q d -> p (q d)"), out_offset=None, in_=h[:, :],
                            in_offset=bass.IndirectOffsetOnAxis(ap=idx_a[:, s:s + 1], axis=0)).then_inc(s_g[s], 16)

            with pool.Fori(0, NT) as i:
                gathers(i)

        @block.vector
        def _(dve):
            steps = Steps(dve, s_dve)
            step = steps.step
            V = nc.vector
            dve.sem_inc(s_wlo, KB)
            dve.sem_inc(s_xlo, 2)
            dve.sem_inc(s_hlo, 4)
            dve.sem_inc(s_cnt, 2)
            dve.sem_inc(s_DT, 2)
            dve.sem_inc(s_look, 2)
            dve.sem_inc(s_w8, 2)
            dve.sem_inc(s_S, HALF)
            dve.sem_inc(s_acc, BANKS)
            dve.sem_inc(s_x2lo, 1)
            dve.sem_inc(s_selfa, 1)
            for made in (V.memset(onesc, 1.0), V.memset(onesk[:], 1.0), V.memset(pos, 0.0)):
                made.then_inc(s_dve, 1)
            steps.count += 3

            def w_low(dest, high, g, k):
                dve.wait_ge(s_whi, g + k + 1)
                V.scalar_tensor_tensor(out=dest, in0=psH[k][:], scalar=SW, in1=high,
                                       op0=ALU.mult, op1=ALU.subtract).then_inc(s_wlo, 1)

            def x_low(j, t):
                dve.wait_ge(s_xhi, t + 1)
                V.scalar_tensor_tensor(out=xT[:, j, 1, :], in0=psT[j][:], scalar=SX, in1=xT[:, j, 0, :],
                                       op0=ALU.mult, op1=ALU.subtract).then_inc(s_xlo, 1)

            def h_low(j, t, after=None, before=None):
                for r in range(R):
                    if before:
                        before(r)
                    dve.wait_ge(s_hhi, R * t + r + 1)
                    V.scalar_tensor_tensor(out=hst[:, j, r, 1, :], in0=psH[r % 4][:], scalar=SH / (SX * SW),
                                           in1=hst[:, j, r, 0, :], op0=ALU.mult, op1=ALU.subtract).then_inc(s_hlo, 1)
                    if after:
                        after(r)

            def pair(u, after=None, before=None):
                x_low(1, 2 * u + 1)
                h_low(0, 2 * u, after and (lambda r: after(0, r)), before and (lambda r: before(0, r)))
                x_low(0, 2 * u + 2)
                h_low(1, 2 * u + 1, after and (lambda r: after(1, r)), before and (lambda r: before(1, r)))

            def high_low(r, c):
                return [w_all[:, ds(r, 1), k, c, :].rearrange("p r d -> p (r d)") for k in range(KB)]

            def next_and_h_low(r, j):
                for k in range(KB):
                    w_low(high_low(r + 1, 1)[k], high_low(r + 1, 0)[k], (r + 1) * KB, k)
                dve.wait_ge(s_hhi, r + 1)
                low, high = (hst[:, 0, ds(r, 1), c, :].rearrange("p r d -> p (r d)") for c in (1, 0))
                V.scalar_tensor_tensor(out=low, in0=psM[j][:], scalar=SH / (SX * SW), in1=high,
                                       op0=ALU.mult, op1=ALU.subtract).then_inc(s_hlo, 1)

            x_low(0, 0)
            for k in range(KB):
                w_low(w_all[:, 0, k, 1, :], w_all[:, 0, k, 0, :], 0, k)
            with dve.Fori(0, R // 2 - 1) as u:
                next_and_h_low(2 * u, 0)
                next_and_h_low(2 * u + 1, 1)
            next_and_h_low(R - 2, 0)
            dve.wait_ge(s_const, 3)
            dve.wait_ge(s_w[0], 16 * (R // 2 + 1))
            for b in range(KB):
                block_b = wst[:, 0, b, b * P:(b + 1) * P]
                V.tensor_tensor(block_b, block_b, ident[:], ALU.add).then_inc(s_folded, 1)
            next_and_h_low(R - 1, 1)
            x_low(1, 1)
            dve.wait_ge(s_edges, 96)
            dve.wait_ge(s_iota, 4)
            step(V.tensor_scalar(tmp_i, dst_i, 7, None, op0=ALU.arith_shift_right))
            step(V.tensor_copy(key, tmp_i))
            step(V.tensor_scalar(tmp_i, dst_i, P - 1, None, op0=ALU.bitwise_and))
            step(V.scalar_tensor_tensor(out=rec, in0=src_i, scalar=float(R), in1=et_i, op0=ALU.mult, op1=ALU.add))
            step(V.scalar_tensor_tensor(out=rec, in0=tmp_i[:, 0:C], scalar=65536.0, in1=rec, op0=ALU.mult, op1=ALU.add))
            step(V.tensor_scalar(val, key[:, 0:C], float(NT), INVALID, op0=ALU.is_equal, op1=ALU.mult))
            step(V.tensor_tensor(rec, rec, val, ALU.add))
            dve.sem_inc(s_rec, 1)
            step(V.tensor_tensor(onek, key[:, 0:C], key[:, 1:C + 1], ALU.is_gt))
            step(V.tensor_reduce(unsorted[:], onek, op=ALU.max, axis=AX.X))
            def count_keys(u, j, r):
                for k in ((r, KPT - 1) if r == R - 1 else (r,)):
                    at = ds(2 * KPT * u + KPT * j + k, 1)
                    step(V.tensor_scalar(onek, key[:, 0:C], iota_k[:, at], 0.0, op0=ALU.is_equal, op1=ALU.add,
                                         accum_out=hist[:, at]))

            x_low(0, 2)

            def first_keys(r):
                count_keys(0, 0, r)
                count_keys(0, 1, r)

            h_low(1, 1, first_keys)
            with dve.Fori(1, HIST_END) as u:
                steps.enter(u - 1, 2 * KPT)
                pair(u, lambda j, r: count_keys(u, j, r))
                steps.leave(HIST_END - 1)
            dve.sem_inc(s_hist, 1)
            def over_k(t):
                return t.unsqueeze(1).broadcast_to([P, CG, NT])

            def over_g(t):
                return t.unsqueeze(2).broadcast_to([P, CG, NT])

            def chunk_tables(j, r):
                if j == 0:
                    return
                if r == 0:
                    dve.wait_ge(s_tot, 1)
                    step(V.tensor_copy(total[:], psM[0][:, 0:K]))
                    step(V.tensor_copy(base[:], psM[1][:, 0:K]))
                    step(V.tensor_copy(unsorted_i[:], psM[0][0:1, K:K + 1]))
                    step(V.tensor_scalar(total_i[:], total[:], float(P - 1), None, op0=ALU.add))
                elif r == 1:
                    step(V.tensor_scalar(total_i[:], total_i[:], 7, None, op0=ALU.arith_shift_right))
                    step(V.tensor_copy(nchunk[:], total_i[:]))
                    step(V.tensor_tensor_scan(cend[:], onesk[:], nchunk[:], 0.0, ALU.mult, ALU.add))
                    step(V.tensor_tensor_scan(eend[:], onesk[:], total[:], 0.0, ALU.mult, ALU.add))
                elif r == 2:
                    step(V.tensor_tensor(total[:], eend[:], total[:], ALU.subtract))
                    step(V.tensor_tensor(nchunk[:], cend[:], nchunk[:], ALU.subtract))
                    step(V.scalar_tensor_tensor(out=base[:], in0=base[:], scalar=-1.0, in1=total[:], op0=ALU.add, op1=ALU.add))
                    step(V.scalar_tensor_tensor(out=lag[:], in0=nchunk[:], scalar=-float(P), in1=total[:], op0=ALU.mult, op1=ALU.add))
                elif r == 3:
                    step(V.tensor_tensor(cmp[:, 0], over_g(chunk_of[:]), over_k(cend[:, 0:NT]), ALU.is_ge))
                    step(V.tensor_reduce(ctile[:], cmp[:, 0], op=ALU.add, axis=AX.X))
                elif r == 4:
                    step(V.tensor_tensor(cmp[:, 0], over_g(ctile[:]), over_k(iota_k[:, 0:NT]), ALU.is_equal))
                    step(V.tensor_tensor(cmp[:, 1], cmp[:, 0], over_k(lag[:, 0:NT]), ALU.mult))
                elif r == 5:
                    step(V.tensor_reduce(estart[:], cmp[:, 1], op=ALU.add, axis=AX.X))
                    step(V.scalar_tensor_tensor(out=estart[:], in0=chunk_of[:], scalar=float(P), in1=estart[:], op0=ALU.mult, op1=ALU.add))
                    step(V.tensor_scalar(estart[:], estart[:], float(C * P), None, op0=ALU.min))
                    step(V.tensor_copy(estart_i[:], estart[:]))
                elif r == 6:
                    step(V.tensor_tensor(cmp[:, 1], cmp[:, 0], over_k(eend[:, 0:NT]), ALU.mult))
                    step(V.tensor_reduce(nvalid[:], cmp[:, 1], op=ALU.add, axis=AX.X))
                    step(V.tensor_tensor(nvalid[:], nvalid[:], estart[:], ALU.subtract))
                elif r == 7:
                    step(V.tensor_scalar(ctile[:], ctile[:], float(NT - 1), None, op0=ALU.min))
                    for g in range(CG):
                        V.tensor_scalar(diag[:, g, :], ident[:], ctile[:, g:g + 1], None, op0=ALU.mult).then_inc(s_dve, 1)
                    steps.count += CG - 1
                    step(None)
                    dve.sem_inc(s_tab, 1)

            pair(HIST_END, chunk_tables)
            is_unsorted = dve.value_load(unsorted_i[0:1, 0:1], min_val=0, max_val=P)
            with dve.If(is_unsorted > 0):
                sort = Steps(dve, s_dveu)
                with dve.Fori(0, K) as k:
                    sort.enter(k, 4)
                    sort.step(V.tensor_scalar(onek, key[:, 0:C], iota_k[:, ds(k, 1)], None, op0=ALU.is_equal))
                    sort.step(V.tensor_tensor_scan(cum, onesc, onek, 0.0, ALU.mult, ALU.add))
                    sort.step(V.scalar_tensor_tensor(out=val, in0=cum, scalar=base[:, ds(k, 1)], in1=onek,
                                                     op0=ALU.add, op1=ALU.mult))
                    sort.step(V.tensor_tensor(pos, pos, val, ALU.add))
                    sort.leave(K)
                sort.step(V.tensor_copy(pos_i, pos))
                dve.sem_inc(s_pos, 1)
            with dve.Else():
                dve.nop()
            tiles_p = tile_i.rearrange("o (m b) -> o b m", b=2)
            first, second = run[0:1, 0:STREAM], run[0:1, STREAM:2 * STREAM]
            shared = run[0:1, STREAM - 1:STREAM]
            valid3 = relT.rearrange("p (g e) -> p g e", g=CG)

            def neighbours(j, r):
                if j == 0:
                    return
                if r == 0:
                    dve.wait_ge(s_tiles, 1)
                    step(V.tensor_copy(run[:, 0:4 * P], psM[0][:]))
                elif r == 1:
                    step(V.tensor_copy(run[:, 4 * P:NCP], psM[1][:, 0:NCP - 4 * P]))
                elif r == 2:
                    step(V.tensor_copy(tiles_p[:, 0], first))
                    step(V.tensor_copy(shared_i[:], shared))
                    step(V.tensor_scalar(gap[:], shared, -1.0, float(NT), op0=ALU.mult, op1=ALU.add))
                elif r == 3:
                    step(V.tensor_scalar(relT[0:1, 0:STREAM], second, shared, None, op0=ALU.is_equal))
                    step(V.scalar_tensor_tensor(out=tiles_p[:, 1], in0=relT[0:1, 0:STREAM], scalar=gap[:],
                                                in1=second, op0=ALU.mult, op1=ALU.add))
                elif r == 4:
                    step(V.memset(same_prev, 0.0))
                    step(V.memset(same_next, 0.0))
                elif r == 5:
                    step(V.tensor_tensor(same_prev[:, 1:NCP], run[:, 1:NCP], run[:, 0:NCP - 1], ALU.is_equal))
                elif r == 6:
                    step(V.tensor_tensor(same_next[:, 0:NCP - 1], run[:, 0:NCP - 1], run[:, 1:NCP], ALU.is_equal))
                elif r == 7:
                    step(V.tensor_tensor(valid3, iota_row[:].unsqueeze(1).broadcast_to([P, CG, P]),
                                         nvalid[:].unsqueeze(2).broadcast_to([P, CG, P]), ALU.is_lt))

            pair(HIST_END + 1, neighbours)
            dve.wait_ge(s_slotg, 16 * CG)
            step(V.scalar_tensor_tensor(out=slotc, in0=slotc, scalar=-INVALID, in1=relT, op0=ALU.add, op1=ALU.mult))
            step(V.tensor_scalar(slotc, slotc, INVALID, None, op0=ALU.add))
            step(V.tensor_copy(slotc_i, slotc))
            step(V.tensor_scalar(slotc_i, slotc_i, 16, None, op0=ALU.arith_shift_right))
            step(V.tensor_copy(rowc, slotc_i))
            dve.sem_inc(s_rowc, 1)

            def decode(j, r):
                if j == 0:
                    return
                if r == 0:
                    dve.wait_ge(s_slotT, 1)
                    step(V.tensor_copy(rec_i[:, 0:4 * P], psM[0][:]))
                elif r == 1:
                    step(V.tensor_copy(rec_i[:, 4 * P:NCP], psM[1][:, 0:NCP - 4 * P]))
                elif r == 2:
                    step(V.memset(gidx[:, CPT * NT:], 0))
                    step(V.tensor_scalar(gidx[:, 0:CPT * NT].rearrange("p (m b) -> p b m", b=2),
                                         rec_i[:, 0:2 * STREAM].rearrange("p (b m) -> p b m", b=2), 65535, None, op0=ALU.bitwise_and))
                elif r == 3:
                    step(V.tensor_scalar(slotc_i, rec_i, R - 1, None, op0=ALU.bitwise_and))
                elif r == 4:
                    dve.wait_ge(s_recst, 32)
                    step(V.tensor_copy(relK, slotc_i))
                elif r == 5:
                    step(V.tensor_scalar(slotc_i, rec_i, 16, None, op0=ALU.arith_shift_right))
                elif r == 6:
                    step(V.tensor_copy(rowT[:], slotc_i))
                elif r == 7:
                    step(V.memset(rowP[:, CPT * NT:], 0.0))
                    step(V.tensor_copy(rowP[:, 0:CPT * NT].rearrange("p (m b) -> p b m", b=2),
                                       slotc_i[:, 0:2 * STREAM].rearrange("p (b m) -> p b m", b=2)))

            pair(HIST_END + 2, decode)
            dve.wait_ge(s_rowst, 16)

            def rows_one_hot(dest, c0, n, rows=rowT):
                return V.tensor_tensor(dest, rows[:, ds(c0, n)].unsqueeze(2).broadcast_to([P, n, P]),
                                       iota_row[:].unsqueeze(1).broadcast_to([P, n, P]), ALU.is_equal)

            def relations_one_hot(j, g):
                return V.tensor_tensor(relg[:, j], relK[:, ds(g * GC, GC)].unsqueeze(2).broadcast_to([P, GC, R]),
                                       iota_k[:, 0:R].unsqueeze(1).broadcast_to([P, GC, R]), ALU.is_equal)

            with dve.Fori(COUNT, SCAN) as u:
                def one_hots(j, r):
                    if r % 2 == 0:
                        g = 8 * (u - COUNT) + 4 * j + r // 2
                        dve.wait_ge(s_cnt, g + 1)
                        relations_one_hot(r // 2 % 2, g).then_inc(s_D1, 1)
                        rows_one_hot(D1[:, r // 2 % 2], g * GC, GC).then_inc(s_D1, 1)

                pair(u, before=one_hots)
            dve.wait_ge(s_cntc, 2 + NCP // GC)
            dve.wait_ge(s_cnt, 2 + NCP // GC)
            with dve.Fori(SCAN, LOOK) as u:
                steps.enter(u - SCAN, 2 * 8)

                def invert(j, r):
                    rel = 2 * (u - SCAN) + j
                    mine = cnt[:, ds(rel, 1), :].rearrange("p r c -> p (r c)")
                    high = inv[:, ds(rel, 1), 0, :].rearrange("p r c -> p (r c)")
                    low = inv[:, ds(rel, 1), 1, :].rearrange("p r c -> p (r c)")
                    if r == 0:
                        step(V.tensor_tensor_scan(run, same_prev, mine, 0.0, ALU.mult, ALU.add))
                    elif r == 1:
                        step(V.tensor_tensor(tmpc, run, same_next, ALU.mult))
                    elif r == 2:
                        step(V.tensor_tensor(tmpc, run, tmpc, ALU.subtract))
                    elif r == 3:
                        step(V.tensor_tensor_scan(run[:, ::-1], same_next[:, ::-1], tmpc[:, ::-1], 0.0, ALU.mult, ALU.add))
                    elif r == 4:
                        step(V.tensor_scalar(run, run, 1.0, None, op0=ALU.max))
                        step(V.reciprocal(tmpc, run))
                    elif r == 6:
                        step(V.tensor_scalar(high, tmpc, SWT, None, op0=ALU.mult))
                    elif r == 7:
                        step(V.scalar_tensor_tensor(out=low, in0=tmpc, scalar=SWT, in1=high, op0=ALU.mult, op1=ALU.subtract))

                pair(u, invert)
                steps.leave(LOOK - SCAN)
            dve.sem_inc(s_inv, 1)
            with dve.Fori(LOOK, PAIRS) as u:
                steps.enter(u - LOOK, 2 * 8)

                def weights(j, r):
                    g = 8 * (u - LOOK) + 4 * j + r // 2
                    q = r // 2 % 2
                    if r % 2 == 0:
                        dve.wait_ge(s_rb[q], 16 * (4 * (u - LOOK) + 2 * j + r // 4 + 1))
                        dve.wait_ge(s_look, g + 1)
                        V.tensor_scalar(D1[:, q], rows_b[:, q], iota_part[:, 0:1], None, op0=ALU.is_equal).then_inc(s_DT, 1)
                    else:
                        step(relations_one_hot(q, g))
                        dve.wait_ge(s_look, 2 + g + 1)
                        step(V.tensor_tensor(prod, psM[q][:, 0:GC * 2 * R].rearrange("p (c r q) -> p c r q", q=2, r=R),
                                             relg[:, q].unsqueeze(3).broadcast_to([P, GC, R, 2]), ALU.mult))
                        V.tensor_reduce(wgt[:, ds(g * GC, GC), :], prod.rearrange("p c r q -> p c q r"),
                                        op=ALU.add, axis=AX.X).then_inc(s_w8, 1)

                pair(u, weights)
                steps.leave(PAIRS - LOOK)
            dve.wait_ge(s_bias, 16)
            dve.wait_ge(s_w8, 2 + NCP // GC)
            def start_as_bias(t):
                V.tensor_copy(flat(acc[:, ds(t, 1), :]), biasb[:]).then_inc(s_accz, 1)

            V.memset(acc[:, NT, :], 0.0).then_inc(s_accz, 1)
            with dve.Fori(0, EARLY // 4) as i:
                for k in range(4):
                    start_as_bias(2 * UNDER_H + 4 * i + k)
            h_low(0, NT - 1)

            dve.wait_ge(s_h, R * NT)
            rows_one_hot(dgrp[:, 0], 0, HALF, rowP).then_inc(s_D, 1)
            for t in range(2 * UNDER_H + EARLY, LATE):
                start_as_bias(t)
            dve.wait_ge(s_st[1], 16 * PAIRS)
            for t in range(UNDER_H, UNDER_H * 13 // 8):
                start_as_bias(t)
            dve.wait_ge(s_st[0], 16 * (PAIRS + LASTST))
            for t in range(UNDER_H * 5 // 8):
                start_as_bias(t)
            dve.wait_ge(s_accz, NT + 1)
            with dve.Fori(0, NT) as i:
                _, tiles = nc.values_load_multi_w_load_instructions(
                    tile_i[0:1, ds(CPT * i, CPT)], engines=(mybir.EngineType.DVE,), min_val=0, max_val=NT,
                    skip_runtime_bounds_check_because="the chunk tables hold tiles up to NT - 1, and NT for the spare")
                for s in range(CPT):
                    c = CPT * i + s
                    if s % HALF == 0:
                        a = s // HALF
                        dve.wait_ge(s_S, HALF * (2 * i + a + 1))
                        rows_one_hot(dgrp[:, 1 - a], c + HALF, HALF, rowP).then_inc(s_D, 1)
                    dve.wait_ge(s_mm, BANKS + c + 1)
                    dve.wait_ge(s_acc, BANKS - 1 + c)
                    row = flat(acc[:, ds(tiles[s], 1), :])
                    V.scalar_tensor_tensor(out=row, in0=ps2[s % BANKS][:], scalar=1.0 / (SH * SWT), in1=row,
                                           op0=ALU.mult, op1=ALU.add).then_inc(s_acc, 1)
                    if s == 9:
                        dve.wait_ge(s_x2hi, i + 1)
                        V.scalar_tensor_tensor(out=xT[:, 0, 1, :], in0=psT[0][:], scalar=SX, in1=xT[:, 0, 0, :],
                                               op0=ALU.mult, op1=ALU.subtract).then_inc(s_x2lo, 1)
                    if s == 16:
                        dve.wait_ge(s_self, i + 1)
                        dve.wait_ge(s_acc, BANKS + c + 1)
                        own = flat(acc[:, ds(i, 1), :])
                        V.scalar_tensor_tensor(out=own, in0=psT[1][:], scalar=1.0 / (SX * SW), in1=own,
                                               op0=ALU.mult, op1=ALU.add).then_inc(s_selfa, 1)
                        dve.wait_ge(s_selfa, 1 + i + 1)
            dve.wait_ge(s_acc, BANKS + CPT * NT)
            shared_tile = dve.value_load(shared_i[0:1, 0:1], min_val=0, max_val=NT - 1)
            shared_acc = flat(acc[:, ds(shared_tile, 1), :])
            V.tensor_tensor(shared_acc, shared_acc, acc[:, NT, :], ALU.add).then_inc(s_merged, 1)
            dve.wait_ge(s_merged, 1)
            def moments(lo, hi):
                with dve.Fori(0, (hi - lo) // 4) as i:
                    for j in range(4):
                        t = lo + 4 * i + j
                        V.bn_stats(flat(stats[:, ds(t, 1), :]), flat(acc[:, ds(t, 1), :])).then_inc(s_dve, 1)
                for t in range(lo + (hi - lo) // 4 * 4, hi):
                    V.bn_stats(stats[:, t, :], acc[:, t, :]).then_inc(s_dve, 1)
                steps.count += hi - lo - 1
                step(None)
                m0, m1, q0, q1 = (stats[:, lo:hi, n] for n in (1, 4, 2, 5))
                mu, v, nb = mean[:, lo:hi], var[:, lo:hi], nbias[:, lo:hi]
                step(V.tensor_tensor(nb, m0, m1, ALU.subtract))
                step(V.tensor_tensor(v, q0, q1, ALU.add))
                step(V.scalar_tensor_tensor(out=nb, in0=nb, scalar=0.25, in1=nb, op0=ALU.mult, op1=ALU.mult))
                step(V.scalar_tensor_tensor(out=v, in0=v, scalar=1.0 / D, in1=nb, op0=ALU.mult, op1=ALU.add))
                step(V.tensor_scalar(v, v, EPS, None, op0=ALU.add))
                dve.sem_inc(s_mv, 1)
                step(V.tensor_tensor(mu, m0, m1, ALU.add))
                step(V.tensor_scalar(mu, mu, 0.5, None, op0=ALU.mult))

            def inverses(k, lo, hi):
                mu, rs, nb = mean[:, lo:hi], rstd[:, lo:hi], nbias[:, lo:hi]
                dve.wait_ge(s_std, k)
                step(V.reciprocal(rs, rs))
                step(V.scalar_tensor_tensor(out=nb, in0=mu, scalar=-1.0, in1=rs, op0=ALU.mult, op1=ALU.mult))
                dve.sem_inc(s_rstd, 1)

            def normalise(t):
                row = flat(acc[:, ds(t, 1), :])
                V.tensor_scalar(row, row, mean[:, ds(t, 1)], rstd[:, ds(t, 1)],
                                op0=ALU.subtract, op1=ALU.mult).then_inc(s_y[0], 1)

            moments(0, NORM)
            inverses(1, 0, NORM)
            moments(NORM, NT)
            inverses(2, NORM, NT)
            with dve.Fori(0, (NT - NORM) // 4) as i:
                for j in range(2):
                    normalise(NORM + 4 * i + 2 * j)
            V.tensor_scalar(acc[:, NT - 1, :], acc[:, NT - 1, :], mean[:, NT - 1:NT], rstd[:, NT - 1:NT],
                            op0=ALU.subtract, op1=ALU.mult).then_inc(s_y[0], 1)


class Steps:

    def __init__(self, engine, semaphore):
        self.engine, self.semaphore = engine, semaphore
        self.count, self.before = 0, 0

    def step(self, instruction):
        self.count += 1
        if instruction is not None:
            instruction.then_inc(self.semaphore, 1)
        self.engine.wait_ge(self.semaphore, self.before + self.count)

    def enter(self, i, per):
        self.outside, self.per = self.count, per
        self.before = i * per

    def leave(self, turns):
        assert self.count - self.outside == self.per, (self.count, self.outside, self.per)
        self.count = self.outside + turns * self.per
        self.before = 0


def kernel(**inputs):
    import numpy as np
    import concourse.bacc as bacc
    from concourse.bass_utils import run_bass_kernel_spmd

    nc = bacc.Bacc("TRN2", target_bir_lowering=False, num_devices=1)
    arrays, args = {}, []
    for name in ("x", "src", "dst", "edge_type_8", "L0_gnn_W_self", "L0_gnn_W_rel", "L0_gnn_bias"):
        a = np.ascontiguousarray(inputs[name])
        arrays["in_" + name] = a
        args.append(nc.dram_tensor("in_" + name, a.shape, mybir.dt.from_np(a.dtype), kind="ExternalInput").ap())
    out = nc.dram_tensor("out", arrays["in_x"].shape, mybir.dt.float32, kind="ExternalOutput").ap()
    build_gnn(nc, *args, out)
    return run_bass_kernel_spmd(nc, [arrays], core_ids=[0]).results[0]["out"]
```
